# Optimizing a Trainium2 kernel written in Bass

```python
import numpy as np
import jax
import jax.numpy as jnp

def _softmax(x, axis=-1):
    return jax.nn.softmax(x, axis=axis)

def _gelu(x):
    return jax.nn.gelu(x, approximate=True)

def _silu(x):
    return jax.nn.silu(x)

def _sigmoid(x):
    return jax.nn.sigmoid(x)

def _layernorm(x, axis=-1, eps=1e-05):
    m = jnp.mean(x, axis=axis, keepdims=True)
    v = jnp.var(x, axis=axis, keepdims=True)
    return (x - m) / jnp.sqrt(v + eps)

def _scatter_add(tgt, idx, src, axis=0):
    return tgt.at[idx].add(src)

def _segment_sum(src, seg, n):
    return jax.ops.segment_sum(src, seg, n)
kernel_name = 'mk_seq_postln_d2_jaxref_r8_db907c'

def setup_inputs(seed: int=0):
    np.random.seed(seed)
    _w = jnp.asarray

    def _L0_attn_setup():
        import jax, jax.numpy as jnp
        import numpy as np
        HEADS = 16
        DIMS = [64, 64, 64, 64]
        EPS = 0.0001
        P_POW = 2

        def _cdist(Q, K):
            q2 = jnp.sum(Q * Q, axis=-1)
            k2 = jnp.sum(K * K, axis=-1)
            qk = jnp.einsum('hbtd,hbsd->hbts', Q, K)
            d2 = q2[..., :, None] + k2[..., None, :] - 2.0 * qk
            return jnp.sqrt(jnp.maximum(d2, 0.0))
        key = jax.random.key(seed)
        ks = jax.random.split(key, 4)
        b, t, d_in = (2, 256, 128)
        d_proj = HEADS * sum(DIMS)
        X = jax.random.normal(ks[0], (b, t, d_in), dtype=jnp.float32)
        W_in = jax.random.normal(ks[1], (d_in, d_proj), dtype=jnp.float32) * d_in ** (-0.5)
        b_in = jnp.zeros((d_proj,), dtype=jnp.float32)
        W_out = jax.random.normal(ks[2], (HEADS * DIMS[2], d_in), dtype=jnp.float32) * (HEADS * DIMS[2]) ** (-0.5)
        b_out = jnp.zeros((d_in,), dtype=jnp.float32)
        return {'X': X, 'W_in': W_in, 'b_in': b_in, 'W_out': W_out, 'b_out': b_out}
    _L0_attn_in = _L0_attn_setup()

    def _L0_ffn_setup():
        import jax, jax.numpy as jnp
        import numpy as np
        CAP_FACTOR = 1.5
        key = jax.random.key(seed)
        ks = jax.random.split(key, 6)
        E, S, D, M = (48, 4, 128, 128)
        K = D // S
        x = jax.random.normal(ks[0], (4, 512, D), dtype=jnp.float32)
        Wr = jax.random.normal(ks[1], (E, D), dtype=jnp.float32) * 0.02
        W1 = jax.random.normal(ks[2], (E, S, D, M), dtype=jnp.float32) * (1.0 / np.sqrt(D))
        b1 = jnp.zeros((E, S, M), dtype=jnp.float32)
        W2 = jax.random.normal(ks[3], (E, S, M, K), dtype=jnp.float32) * (1.0 / np.sqrt(M))
        b2 = jnp.zeros((E, S, K), dtype=jnp.float32)
        return {'x': x, 'Wr': Wr, 'W1': W1, 'b1': b1, 'W2': W2, 'b2': b2}
    _L0_ffn_in = _L0_ffn_setup()

    def _L1_attn_setup():
        import jax, jax.numpy as jnp
        import numpy as np
        import math
        D = 128
        H = 16
        DH = D // H

        def sinusoidal_pe(length, d):
            pos = jnp.arange(length, dtype=jnp.float32)[:, None]
            div = jnp.exp(jnp.arange(0, d, 2, dtype=jnp.float32) * (-math.log(10000.0) / d))
            ang = pos * div
            return jnp.stack([jnp.sin(ang), jnp.cos(ang)], axis=-1).reshape(length, d)

        def _relative_shift(pos_score):
            B, Hh, S1, S2 = pos_score.shape
            padded = jnp.concatenate([jnp.zeros((B, Hh, S1, 1), pos_score.dtype), pos_score], axis=-1)
            padded = padded.reshape(B, Hh, S2 + 1, S1)
            return padded[:, :, 1:].reshape(B, Hh, S1, S2)
        key = jax.random.key(seed)
        ks = jax.random.split(key, 12)
        s = 0.02
        x = jax.random.normal(ks[0], (2, 256, D), dtype=jnp.float32)
        return {'x': x, 'ln_g': jnp.ones((D,), jnp.float32), 'ln_b': jnp.zeros((D,), jnp.float32), 'Wq': jax.random.normal(ks[1], (D, D), jnp.float32) * s, 'bq': jnp.zeros((D,), jnp.float32), 'Wk': jax.random.normal(ks[2], (D, D), jnp.float32) * s, 'bk': jnp.zeros((D,), jnp.float32), 'Wv': jax.random.normal(ks[3], (D, D), jnp.float32) * s, 'bv': jnp.zeros((D,), jnp.float32), 'Wp': jax.random.normal(ks[4], (D, D), jnp.float32) * s, 'Wo': jax.random.normal(ks[5], (D, D), jnp.float32) * s, 'bo': jnp.zeros((D,), jnp.float32), 'u_bias': jax.random.normal(ks[6], (H, DH), jnp.float32) * 0.05, 'v_bias': jax.random.normal(ks[7], (H, DH), jnp.float32) * 0.05}
    _L1_attn_in = _L1_attn_setup()

    def _L1_ffn_setup():
        import jax, jax.numpy as jnp
        import numpy as np
        B, S, D, E = (4, 512, 128, 8)
        key = jax.random.key(seed)
        ks = jax.random.split(key, 6)
        scale = 1.0 / np.sqrt(D)
        return {'tokens': jax.random.normal(ks[0], (B, S, D), dtype=jnp.float32), 'gate_w': jax.random.normal(ks[1], (D, E), dtype=jnp.float32) * scale, 'w0': jax.random.normal(ks[2], (D, D), dtype=jnp.float32) * scale, 'b0': jax.random.normal(ks[3], (D,), dtype=jnp.float32) * 0.01, 'w1': jax.random.normal(ks[4], (D, D), dtype=jnp.float32) * scale, 'b1': jax.random.normal(ks[5], (D,), dtype=jnp.float32) * 0.01}
    _L1_ffn_in = _L1_ffn_setup()
    _d = {'L0_attn_X': _L0_attn_in['X'], 'L0_attn_W_in': _L0_attn_in['W_in'], 'L0_attn_b_in': _L0_attn_in['b_in'], 'L0_attn_W_out': _L0_attn_in['W_out'], 'L0_attn_b_out': _L0_attn_in['b_out'], 'L0_ffn_Wr': _L0_ffn_in['Wr'], 'L0_ffn_W1': _L0_ffn_in['W1'], 'L0_ffn_b1': _L0_ffn_in['b1'], 'L0_ffn_W2': _L0_ffn_in['W2'], 'L0_ffn_b2': _L0_ffn_in['b2'], 'L1_attn_ln_g': _L1_attn_in['ln_g'], 'L1_attn_ln_b': _L1_attn_in['ln_b'], 'L1_attn_Wq': _L1_attn_in['Wq'], 'L1_attn_bq': _L1_attn_in['bq'], 'L1_attn_Wk': _L1_attn_in['Wk'], 'L1_attn_bk': _L1_attn_in['bk'], 'L1_attn_Wv': _L1_attn_in['Wv'], 'L1_attn_bv': _L1_attn_in['bv'], 'L1_attn_Wp': _L1_attn_in['Wp'], 'L1_attn_Wo': _L1_attn_in['Wo'], 'L1_attn_bo': _L1_attn_in['bo'], 'L1_attn_u_bias': _L1_attn_in['u_bias'], 'L1_attn_v_bias': _L1_attn_in['v_bias'], 'L1_ffn_gate_w': _L1_ffn_in['gate_w'], 'L1_ffn_w0': _L1_ffn_in['w0'], 'L1_ffn_b0': _L1_ffn_in['b0'], 'L1_ffn_w1': _L1_ffn_in['w1'], 'L1_ffn_b1': _L1_ffn_in['b1']}
    _x0 = _d['L0_attn_X']
    _d['L0_attn_X'] = jax.random.normal(jax.random.fold_in(jax.random.key(seed), 1), (8, 512, 128), dtype=_x0.dtype)
    del _x0
    return _d

def reference(L0_attn_X, L0_attn_W_in, L0_attn_b_in, L0_attn_W_out, L0_attn_b_out, L0_ffn_Wr, L0_ffn_W1, L0_ffn_b1, L0_ffn_W2, L0_ffn_b2, L1_attn_ln_g, L1_attn_ln_b, L1_attn_Wq, L1_attn_bq, L1_attn_Wk, L1_attn_bk, L1_attn_Wv, L1_attn_bv, L1_attn_Wp, L1_attn_Wo, L1_attn_bo, L1_attn_u_bias, L1_attn_v_bias, L1_ffn_gate_w, L1_ffn_w0, L1_ffn_b0, L1_ffn_w1, L1_ffn_b1):

    def _L0_attn_ref(X, W_in, b_in, W_out, b_out):
        import jax, jax.numpy as jnp
        import numpy as np
        HEADS = 16
        DIMS = [64, 64, 64, 64]
        EPS = 0.0001
        P_POW = 2

        def _cdist(Q, K):
            q2 = jnp.sum(Q * Q, axis=-1)
            k2 = jnp.sum(K * K, axis=-1)
            qk = jnp.einsum('hbtd,hbsd->hbts', Q, K)
            d2 = q2[..., :, None] + k2[..., None, :] - 2.0 * qk
            return jnp.sqrt(jnp.maximum(d2, 0.0))
        b, t, _ = X.shape
        P = X @ W_in + b_in
        P = P.reshape(b, t, HEADS, sum(DIMS))
        P = jnp.transpose(P, (2, 0, 1, 3))
        splits = np.cumsum(DIMS)[:-1]
        Q, K, V, G = jnp.split(P, splits, axis=-1)
        W = jnp.power(EPS + _cdist(Q, K), -P_POW)
        W = W / (EPS + jnp.sum(W, axis=-1, keepdims=True))
        A = jnp.einsum('hbts,hbse->hbte', W, V)
        H = G * A
        H = jnp.transpose(H, (1, 2, 0, 3)).reshape(b, t, HEADS * DIMS[2])
        return H @ W_out + b_out

    def _L0_ffn_ref(x, Wr, W1, b1, W2, b2):
        import jax, jax.numpy as jnp
        import numpy as np
        CAP_FACTOR = 1.5
        orig_shape = x.shape
        D = x.shape[-1]
        E = Wr.shape[0]
        xf = x.reshape(-1, D)
        T = xf.shape[0]
        cap = int(CAP_FACTOR * T / E)
        logits = xf @ Wr.T
        vals, idx = jax.lax.top_k(logits.T, cap)
        w = jax.nn.softmax(vals, axis=-1)
        xg = xf[idx]
        h = jax.nn.gelu(jnp.einsum('ecd,esdm->ecsm', xg, W1) + b1[:, None], approximate=False)
        y = jnp.einsum('ecsm,esmk->ecsk', h, W2) + b2[:, None]
        y = y.reshape(E, cap, D) * w[..., None]
        out = jnp.zeros_like(xf).at[idx.reshape(-1)].add(y.reshape(-1, D))
        return out.reshape(orig_shape)

    def _L1_attn_ref(x, ln_g, ln_b, Wq, bq, Wk, bk, Wv, bv, Wp, Wo, bo, u_bias, v_bias):
        import jax, jax.numpy as jnp
        import numpy as np
        import math
        D = 128
        H = 16
        DH = D // H

        def sinusoidal_pe(length, d):
            pos = jnp.arange(length, dtype=jnp.float32)[:, None]
            div = jnp.exp(jnp.arange(0, d, 2, dtype=jnp.float32) * (-math.log(10000.0) / d))
            ang = pos * div
            return jnp.stack([jnp.sin(ang), jnp.cos(ang)], axis=-1).reshape(length, d)

        def _relative_shift(pos_score):
            B, Hh, S1, S2 = pos_score.shape
            padded = jnp.concatenate([jnp.zeros((B, Hh, S1, 1), pos_score.dtype), pos_score], axis=-1)
            padded = padded.reshape(B, Hh, S2 + 1, S1)
            return padded[:, :, 1:].reshape(B, Hh, S1, S2)
        B, S, Dm = x.shape
        dh = Dm // H
        scale = dh ** (-0.5)
        pe = sinusoidal_pe(S, Dm)
        mu = jnp.mean(x, axis=-1, keepdims=True)
        var = jnp.var(x, axis=-1, keepdims=True)
        xn = (x - mu) / jnp.sqrt(var + 1e-05) * ln_g + ln_b
        q = (xn @ Wq + bq).reshape(B, S, H, dh)
        k = (xn @ Wk + bk).reshape(B, S, H, dh)
        v = (xn @ Wv + bv).reshape(B, S, H, dh)
        p = (pe @ Wp).reshape(S, H, dh)
        content = jnp.einsum('bihd,bjhd->bhij', q + u_bias, k)
        pos = jnp.einsum('bihd,jhd->bhij', q + v_bias, p)
        pos = _relative_shift(pos)
        attn = jax.nn.softmax((content + pos) * scale, axis=-1)
        head = jnp.einsum('bhij,bjhd->bihd', attn, v).reshape(B, S, Dm)
        return head @ Wo + bo

    def _L1_ffn_ref(tokens, gate_w, w0, b0, w1, b1):
        import jax, jax.numpy as jnp
        import numpy as np
        B, S, D, E = (4, 512, 128, 8)
        b, s, d = tokens.shape
        logits = jnp.einsum('bsd,de->bse', tokens, gate_w)
        weights = jax.nn.softmax(logits, axis=-1)
        topk_w, topk_idx = jax.lax.top_k(weights, 2)
        x = tokens.reshape(b * s, d)
        fw = topk_w.reshape(b * s, 2)
        fidx = topk_idx.reshape(b * s, 2)
        e0 = jax.nn.silu(x @ w0.T + b0)
        e1 = jax.nn.silu(x @ w1.T + b1)
        m0 = (fidx[:, 0:1] == 0).astype(x.dtype)
        m1 = (fidx[:, 1:2] == 1).astype(x.dtype)
        out = e0 * fw[:, 0:1] * m0 + e1 * fw[:, 1:2] * m1
        return out.reshape(b, s, d)
    x = L0_attn_X
    x = _layernorm(x + _L0_attn_ref(x, L0_attn_W_in, L0_attn_b_in, L0_attn_W_out, L0_attn_b_out), axis=-1)
    x = _layernorm(x + _L0_ffn_ref(x, L0_ffn_Wr, L0_ffn_W1, L0_ffn_b1, L0_ffn_W2, L0_ffn_b2), axis=-1)
    x = _layernorm(x + _L1_attn_ref(x, L1_attn_ln_g, L1_attn_ln_b, L1_attn_Wq, L1_attn_bq, L1_attn_Wk, L1_attn_bk, L1_attn_Wv, L1_attn_bv, L1_attn_Wp, L1_attn_Wo, L1_attn_bo, L1_attn_u_bias, L1_attn_v_bias), axis=-1)
    x = _layernorm(x + _L1_ffn_ref(x, L1_ffn_gate_w, L1_ffn_w0, L1_ffn_b0, L1_ffn_w1, L1_ffn_b1), axis=-1)
    return x

_drawn_inputs = setup_inputs


def setup_inputs(seed=0):
    import zlib

    import numpy as np

    out = dict(_drawn_inputs(seed))
    spreads = {'L0_attn_b_in': (0.0, 0.1),
     'L0_attn_b_out': (0.0, 0.1),
     'L0_ffn_b1': (0.0, 2.0),
     'L0_ffn_b2': (0.0, 2.0),
     'L1_attn_ln_g': (1.0, 0.6),
     'L1_attn_ln_b': (0.0, 0.8),
     'L1_attn_bq': (0.0, 0.8),
     'L1_attn_bk': (0.0, 2.0),
     'L1_attn_bv': (0.0, 0.305),
     'L1_attn_bo': (0.0, 0.1)}
    factors = {'L0_ffn_Wr': 6.324,
     'L0_ffn_W1': 6.742,
     'L0_ffn_W2': 5.988,
     'L1_attn_Wq': 8.0,
     'L1_attn_Wk': 8.0,
     'L1_attn_Wv': 5.742,
     'L1_attn_Wp': 8.0,
     'L1_attn_u_bias': 8.0,
     'L1_attn_v_bias': 8.0,
     'L1_ffn_b0': 64.0,
     'L1_ffn_b1': 64.0}
    for name, (base, spread) in spreads.items():
        noise = np.random.default_rng([zlib.crc32(name.encode()), seed]).standard_normal(out[name].shape)
        drawn = base * np.exp(spread * noise) if base else spread * noise
        out[name] = jnp.asarray(drawn.astype(out[name].dtype))
    for name, factor in factors.items():
        out[name] = (out[name] * factor).astype(out[name].dtype)
    return out
```

```python
from contextlib import ExitStack

import numpy as np
import concourse.bass as bass
from concourse import mybir

ALU = mybir.AluOpType
ACT = mybir.ActivationFunctionType
F32 = mybir.dt.float32
U32 = mybir.dt.uint32
AX_X = mybir.AxisListType.X

P = 128
LN_EPS = 1e-5
POW_EPS = 1e-4


class Line:

    def __init__(self, name, new_sem, in_order=False):
        self.name, self.new_sem, self.in_order, self.last = name, new_sem, in_order, None
        self.queue, self.waited = [], {}
        self.stage("start")

    def stage(self, stage):
        self.sem, self.count = self.new_sem(f"{self.name}_{stage}"), 0

    def wait(self, *tickets):
        for t in tickets:
            if t is None:
                continue
            sem, value = t
            if self.waited.get(sem.name, 0) < value:
                self.waited[sem.name] = value
                self.queue.append(lambda e, s=sem, v=value: e.wait_ge(s, v))

    def do(self, emit, *needs, signal=True):
        self.wait(*needs, self.last if self.in_order else None)
        if not signal:
            self.queue.append(emit)
            return None
        self.count += 1
        sem = self.sem
        self.queue.append(lambda e: emit(e).then_inc(sem, 1))
        self.last = (sem, self.count)
        return self.last

    def dma(self, lane, out, in_, *needs):
        self.wait(*needs)
        lane.total += 16
        self.queue.append(lambda e: e.dma_start(out, in_).then_inc(lane.sem, 16))
        return (lane.sem, lane.total)

    def play(self, engine):
        for step in self.queue:
            step(engine)


class Lane:

    def __init__(self, sem):
        self.sem, self.total = sem, 0


class Machine:

    def __init__(self, nc, ctx):
        self.nc, self.ctx = nc, ctx
        self.pe = Line("pe", self.semaphore)
        self.act = Line("act", self.semaphore)
        self.dve = Line("dve", self.semaphore)
        self.pool = Line("pool", self.semaphore, in_order=True)
        self.sp = Line("sp", self.semaphore)
        self.stage_ctx = None

    def semaphore(self, name):
        return self.ctx.enter_context(self.nc.semaphore(name))

    def lane(self, name):
        return Lane(self.semaphore(name))

    def sb(self, name, shape, dt=F32):
        return self.ctx.enter_context(self.nc.sbuf_tensor(name, shape, dt))

    def stage_sb(self, name, shape, dt=F32):
        return self.stage_ctx.enter_context(self.nc.sbuf_tensor(name, shape, dt))

    def stage(self, name):
        for line in (self.pe, self.act, self.dve, self.pool, self.sp):
            line.stage(name)

    def close_stage(self):
        lines = (self.pe, self.act, self.dve, self.pool)
        last = [(line.sem, line.count) for line in lines if line.count]
        for line in lines + (self.sp,):
            line.wait(*[t for t in last if t[0] is not line.sem])
            line.wait(*[t for t in last if t[0] is line.sem])

    def matmul(self, out, lhsT, rhs, *needs, start=True, stop=True, signal=True):
        return self.pe.do(lambda e: e.matmul(out, lhsT, rhs, start=start, stop=stop), *needs, signal=signal)

    def transpose(self, out, in_, ident, *needs, signal=True):
        return self.pe.do(lambda e: e.transpose(out, in_, ident), *needs, signal=signal)

    def activate(self, out, in_, func, *needs, **kw):
        return self.act.do(lambda e: e.activation(out, in_, func, **kw), *needs)

    def scalar_op(self, line, out, in_, s1, s2, op0, op1, *needs):
        if op1 is None:
            return line.do(lambda e: e.tensor_scalar(out, in_, s1, None, op0), *needs)
        return line.do(lambda e: e.tensor_scalar(out, in_, s1, s2, op0, op1), *needs)

    def tensor_op(self, line, out, a, b, op, *needs):
        return line.do(lambda e: e.tensor_tensor(out, a, b, op), *needs)

    def copy(self, line, out, in_, *needs):
        return line.do(lambda e: e.tensor_copy(out, in_), *needs)

    def memset(self, line, out, value, *needs):
        return line.do(lambda e: e.memset(out, value), *needs)


def make_constants(m):
    k = m.k = {}
    k["ident"], k["mirror"], k["ones"] = (m.sb(n, [P, P]) for n in ("ident", "mirror", "ones"))
    k["eps"] = m.sb("eps_cols", [P, 4])
    a = m.memset(m.pool, k["ident"][:, :], 0.0)
    b = m.memset(m.pool, k["mirror"][:, :], 0.0)
    m.pool.wait(a, b)
    m.pool.do(lambda e: e.affine_select(out=k["ident"][:, :], in_=k["ident"][:, :], compare_op=ALU.not_equal,
                                        fill=1.0, base=0, pattern=[[-1, P]], channel_multiplier=1))
    m.pool.do(lambda e: e.affine_select(out=k["mirror"][:, :], in_=k["mirror"][:, :], compare_op=ALU.not_equal,
                                        fill=1.0, base=1 - P, pattern=[[1, P]], channel_multiplier=1))
    m.memset(m.pool, k["ones"][:, :], 1.0)
    m.memset(m.pool, k["eps"][:, 0:1], POW_EPS)
    m.memset(m.pool, k["eps"][:, 1:2], LN_EPS)
    k["ready"] = m.memset(m.pool, k["eps"][:, 2:3], 0.0)


def layernorm_rows(m, x, out, tmp, n, *needs, on=None):
    stats, mv, lg, rstd = tmp
    for i in range(n):
        t = m.dve.do(lambda e, i=i: e.bn_stats(stats[:, i, :], x[:, i, :]), *needs)
        needs = ()
    m.dve.wait(t)
    for i in range(n):
        t = m.dve.do(lambda e, i=i: e.bn_aggr(mv[:, i, :], stats[:, i, :]))
    t1 = m.activate(lg[:, 0:n], mv[:, 0:n, 1], ACT.Ln, t, m.k["ready"], bias=m.k["eps"][:, 1:2])
    t2 = m.activate(rstd[:, 0:n], lg[:, 0:n], ACT.Exp, t1, scale=-0.5, bias=m.k["eps"][:, 2:3])
    for i in range(n):
        r = m.scalar_op(m.dve, out[:, i, :], x[:, i, :], mv[:, i, 0:1], rstd[:, i:i + 1],
                        ALU.subtract, ALU.mult, t2)
    return r


def ln_buffers(make, name, n):
    return (make(name + "_stats", [P, n, 6]), make(name + "_mv", [P, n, 2]),
            make(name + "_lg", [P, n]), make(name + "_rstd", [P, n]))


def distance_attention(m, d, x1):
    B, T, D = d["X"].shape
    H, E = 16, 64
    G = 4
    NG = H // G
    NT = T // P
    sb = m.stage_sb
    k = m.k
    W = sb("a_W_in", [P, 4, H, E])
    Wo = sb("a_W_out", [P, H // 2, D])
    brow = sb("a_b_rows", [4 * H, E])
    bcol = sb("a_b_cols", [P, H // 2, 4])
    bk2 = sb("a_bk_m2", [P, H // 2])
    bv = sb("a_bv", [P, H, E])
    bo = sb("a_bo", [P, D])
    pick = sb("a_pick", [P, 2, G])
    X = sb("a_X", [P, 2, NT, D])
    XB = sb("a_XB", [P, NT, D])
    XT = sb("a_XT", [P, 2, T])
    QA = sb("a_QA", [E + 1, 2, G, T])
    KA = sb("a_KA", [E + 1, 2, G, T])
    GT = sb("a_GT", [P, 2, 2, T])
    V = sb("a_V", [P, 2, NT, 2, 3, E])
    SQ = sb("a_SQ", [P, 2, 2, T])
    q2s = sb("a_q2", [G, T])
    k2s = sb("a_k2", [P, 2, NT, G])
    S = sb("a_S", [P, 2, G, NT, T])
    LR = sb("a_LR", [P, T])
    RR = sb("a_RR", [P, T])
    HT = sb("a_HT", [P, H // 2, T])
    Y = sb("a_Y", [P, NT, D])
    tmp = ln_buffers(sb, "a_ln", NT)
    score_ps, pv_ps, prj_ps = m.ps[0:2], m.ps[2], m.ps[3]

    l_w, l_b, l_x = m.lane("a_l_w"), m.lane("a_l_b"), [m.lane(f"a_l_x{i}") for i in range(2)]
    m.sp.dma(l_x[0], X[:, 0, :, :], d["X"][0].rearrange("(n p) d -> p n d", p=P))
    t_x = [(l_x[0].sem, l_x[0].total), None]
    m.sp.dma(l_b, brow[:, :], d["b_in"].rearrange("(r e) -> r e", e=E))
    m.sp.dma(l_b, bv[:, :, :], d["b_in"].rearrange("(a h c e) -> a h c e", a=1, h=H, c=4)[:, :, 2, :]
             .broadcast_to([P, H, E]))
    m.sp.dma(l_b, bo[:, :], d["b_out"].rearrange("(a e) -> a e", a=1).broadcast_to([P, D]))
    t_b = (l_b.sem, l_b.total)
    for c in range(4):
        m.sp.dma(l_w, W[:, c, :, :], d["W_in"].rearrange("p (h c e) -> p h c e", h=H, c=4)[:, :, c, :])
    m.sp.dma(l_w, Wo[:, :, :], d["W_out"].rearrange("(q p) n -> p q n", p=P))
    t_w = (l_w.sem, l_w.total)

    t = m.memset(m.pool, pick[:, :, :], 0.0)
    m.pool.wait(t)
    for pr in range(2):
        for odd in range(2):
            m.memset(m.pool, pick[E * odd:E * odd + E, pr, 2 * pr + odd:2 * pr + odd + 1], 1.0)
    m.memset(m.pool, KA[E:E + 1, :, :, :], 1.0)
    t_const = m.memset(m.pool, V[:, :, :, :, 1, :], 1.0)

    t = m.transpose(prj_ps[0:E, 0, 0:4 * H], brow[:, :], k["ident"][0:4 * H, 0:4 * H], t_b, k["ready"])
    src = prj_ps[0:E, 0, 0:4 * H].rearrange("p (q o c) -> p o q c", o=2, c=4)
    m.copy(m.dve, bcol[0:E, :, :], src[:, 0], t)
    t = m.copy(m.dve, bcol[E:P, :, :], src[:, 1])
    t_bc = m.scalar_op(m.dve, bk2[:, :], bcol[:, :, 1], -2.0, None, ALU.mult, None, t)

    prj_free = [t_bc, None]
    turn = {"prj": 1, "score": 0}
    score_free = [None, None]
    pv_free = [None, None]
    xT_ready, xT_used = {}, {}
    SQ_used = [None, None]
    q2_lane, q2_sent = m.lane("a_l_q2"), [None]
    S_used = [None, None]
    unit_ready, d2_done, w_done, pv_done = {}, {}, {}, {}
    gt_used = {}
    ht_used = [None]
    x_used = {}
    out_lane = [m.lane("a_l_x1d"), m.lane("a_l_acc")]

    def prj_bank():
        i = turn["prj"]
        turn["prj"] = 1 - i
        return i, prj_ps[:, i, :], prj_free[i]

    def load_x(b):
        if b < B and b > 0:
            t_x[b % 2] = m.sp.dma(l_x[b % 2], X[:, b % 2, :, :], d["X"][b].rearrange("(n p) d -> p n d", p=P),
                                  x_used.get(b - 2))

    def transpose_x(b):
        i, bank, free = prj_bank()
        for n in range(NT):
            t = m.transpose(bank[:, n * P:(n + 1) * P], X[:, b % 2, n, :], k["ident"][:, :], t_x[b % 2], free,
                            k["ready"], signal=n == NT - 1)
        xT_ready[b] = m.copy(m.dve, XT[:, b % 2, :], bank, t, xT_used.get(b - 2))
        prj_free[i] = xT_ready[b]

    def project_pair(u, pr):
        b, g = divmod(u, NG)
        s = u % 2
        q = 2 * g + pr
        before = pv_done.get(u - 2)
        for part in (0, 1, 3):
            i, bank, free = prj_bank()
            t = m.matmul(bank, W[:, part, 2 * q:2 * q + 2, :], XT[:, b % 2, :], t_w, xT_ready[b], free)
            if part == 3:
                last = m.scalar_op(m.dve, GT[:, s, pr, :], bank, bcol[:, q, 3:4], None, ALU.add, None, t, t_bc,
                                   gt_used.get(u - 2))
                prj_free[i] = last
                continue
            a = m.activate(SQ[:, part, pr, :], bank, ACT.Square, t, t_bc, SQ_used[part], bias=bcol[:, q, part:part + 1])
            unit_sq[part][pr] = a
            for odd in range(2):
                rows = slice(E * odd, E * odd + E)
                if part == 0:
                    v = m.scalar_op(m.dve, QA[0:E, s, 2 * pr + odd, :], bank[rows, :], bcol[rows, q, 0:1], None,
                                    ALU.add, None, t, t_bc, before, a)
                else:
                    v = m.scalar_op(m.dve, KA[0:E, s, 2 * pr + odd, :], bank[rows, :], -2.0, bk2[rows, q:q + 1],
                                    ALU.mult, ALU.add, t, t_bc, before, a)
            prj_free[i] = v

    unit_sq = [[None, None], [None, None]]

    def project_rest(u):
        b, g = divmod(u, NG)
        s = u % 2
        before = pv_done.get(u - 2)
        i, bank, free = prj_bank()
        for pr in range(2):
            t = m.matmul(bank[0:G, :], pick[:, pr, :], SQ[:, 0, pr, :], unit_sq[0][pr], t_const, free,
                         start=pr == 0, stop=pr == 1, signal=pr == 1)
        SQ_used[0] = t
        t = m.copy(m.dve, q2s[:, :], bank[0:G, :], t, q2_sent[0])
        prj_free[i] = t
        q2_sent[0] = m.sp.dma(q2_lane, QA[E:E + 1, s, :, :].rearrange("a g t -> a (g t)"), q2s[:, :], t, before)
        i, bank, free = prj_bank()
        for n in range(NT):
            for pr in range(2):
                t = m.matmul(bank[:, G * n + 2 * pr:G * n + 2 * pr + 2], SQ[:, 1, pr, n * P:(n + 1) * P],
                             pick[:, 0, 0:2], unit_sq[1][pr], free, signal=n == NT - 1 and pr == 1)
        SQ_used[1] = t
        k2 = m.copy(m.dve, k2s[:, s, :, :], bank[:, 0:G * NT].rearrange("p (n g) -> p n g", g=G), t, before)
        prj_free[i] = k2
        for half in range(2):
            i, bank, free = prj_bank()
            for n in range(2):
                t = m.matmul(bank[:, n * G * E:(n + 1) * G * E], XT[:, b % 2, (2 * half + n) * P:(2 * half + n + 1) * P],
                             W[:, 2, G * g:G * g + G, :], free, signal=n == 1)
            xT_used[b] = t
            for n in range(2):
                src = bank[:, n * G * E:(n + 1) * G * E].rearrange("p (q o e) -> p q o e", q=2, o=2)
                bias = bv[:, G * g:G * g + G, :].rearrange("p (q o) e -> p q o e", o=2)
                t = m.tensor_op(m.dve, V[:, s, 2 * half + n, :, 0:3:2, :], src, bias, ALU.add, t, t_b, before, t_const)
            prj_free[i] = t
        unit_ready[u] = (t, q2_sent[0])

    def distances(u, h):
        s = u % 2
        for half in range(2):
            i = turn["score"]
            turn["score"] = 1 - i
            ps = score_ps[i]
            for n in range(2):
                sl = 2 * half + n
                t = m.matmul(ps[:, n, :], KA[:, s, h, sl * P:(sl + 1) * P], QA[:, s, h, :], *unit_ready[u],
                             score_free[i], t_const)
                v = m.scalar_op(m.dve, S[:, s, h, sl, :], ps[:, n, :], k2s[:, s, sl, h:h + 1], 0.0, ALU.add, ALU.max,
                                t, S_used[s])
            score_free[i] = v
        flat = S[:, s, h, :, :].rearrange("p n t -> p (n t)")
        d2_done[u, h] = m.activate(flat, flat, ACT.Sqrt, v, bias=k["eps"][:, 2:3])

    def weights(u, h):
        s = u % 2
        flat = S[:, s, h, :, :].rearrange("p n t -> p (n t)")
        t = m.activate(flat, flat, ACT.Ln, d2_done[u, h], k["ready"], bias=k["eps"][:, 0:1])
        w_done[u, h] = m.activate(flat, flat, ACT.Exp, t, scale=-2.0, bias=k["eps"][:, 2:3])

    def apply_pair(u, pr):
        b, g = divmod(u, NG)
        s = u % 2
        done = []
        for odd in range(2):
            ps = pv_ps[:, odd, :]
            h = 2 * pr + odd
            for n in range(NT):
                t = m.matmul(ps, V[:, s, n, pr, odd:odd + 2, :], S[:, s, h, n, :], w_done[u, h], pv_free[odd],
                             start=n == 0, stop=n == NT - 1, signal=n == NT - 1)
            done.append(t)
        pv_done[u] = S_used[s] = t
        rows = [slice(0, E), slice(E, P)]
        for odd in range(2):
            t = m.activate(LR[rows[odd], :], pv_ps[rows[1 - odd], odd, :], ACT.Ln, done[odd], lr_used[0],
                           bias=k["eps"][rows[odd], 0:1])
        t = m.activate(RR[:, :], LR[:, :], ACT.Exp, t, rr_used[0], scale=-1.0, bias=k["eps"][:, 2:3])
        lr_used[0] = t
        t = m.tensor_op(m.dve, RR[:, :], RR[:, :], GT[:, s, pr, :], ALU.mult, t)
        gt_used[u] = t
        for odd in range(2):
            v = m.tensor_op(m.dve, HT[rows[odd], 2 * g + pr, :], pv_ps[rows[odd], odd, :], RR[rows[odd], :], ALU.mult,
                            t, done[odd], ht_used[0])
            pv_free[odd] = v
        rr_used[0] = v
        ht_ready[0] = v

    lr_used, rr_used, ht_ready = [None], [None], [None]

    def finish_batch(b):
        t_xb = None
        for n in range(NT):
            t_xb = m.tensor_op(m.pool, XB[:, n, :], X[:, b % 2, n, :], bo[:, :], ALU.add, t_b, t_x[b % 2],
                               y_done[0])
        i, bank, free = prj_bank()
        for n in range(NT):
            for q in range(H // 2):
                t = m.matmul(bank[:, n * P:(n + 1) * P], HT[:, q, n * P:(n + 1) * P], Wo[:, q, :], ht_ready[0], free,
                             start=q == 0, stop=q == H // 2 - 1, signal=q == H // 2 - 1 and n == NT - 1)
        ht_used[0] = t
        x_used[b] = t_xb
        v = m.tensor_op(m.dve, Y[:, :, :], bank.rearrange("p (n c) -> p n c", n=NT), XB[:, :, :], ALU.add, t, t_xb)
        prj_free[i] = v
        y_done[0] = v
        load_x(b + 2)
        o = x1[:, b * NT:(b + 1) * NT, :]
        r = layernorm_rows(m, Y, o, tmp, NT, v)
        rows = slice(b * T, (b + 1) * T)
        m.sp.dma(out_lane[0], m.x1_dram[rows, :].rearrange("(n p) d -> p n d", p=P), o, r)
        m.sp.dma(out_lane[1], m.acc_dram[0][rows, :].rearrange("(n p) d -> p n d", p=P), o, r)

    y_done = [None]

    units = B * NG
    load_x(1)
    transpose_x(0)
    project_pair(0, 0)
    project_pair(0, 1)
    project_rest(0)
    for u in range(units + 1):
        if u < units:
            for h in range(G):
                distances(u, h)
            weights(u, 0)
        if u + 1 < units:
            if (u + 1) % NG == 0:
                transpose_x((u + 1) // NG)
        if u > 0:
            apply_pair(u - 1, 0)
        if u + 1 < units:
            project_pair(u + 1, 0)
        if u < units:
            weights(u, 1)
        if u > 0:
            apply_pair(u - 1, 1)
        if u + 1 < units:
            project_pair(u + 1, 1)
        if u < units:
            weights(u, 2)
        if u + 1 < units:
            project_rest(u + 1)
        if u < units:
            weights(u, 3)
        if u > 0 and (u - 1) % NG == NG - 1:
            finish_batch((u - 1) // NG)
    m.x1_stored = [(l.sem, l.total) for l in out_lane]


def route(m, d, x1):
    E, D = d["Wr"].shape
    T = x1.shape[1] * P
    C = int(1.5 * T / E)
    HALF = T // 2
    k, sb = m.k, m.stage_sb
    assert C == P
    x1T = sb("r_x1T", [P, T])
    Wr = sb("r_Wr", [E, D])
    WrT = sb("r_WrT", [P, 64])
    L = sb("r_L", [P, HALF])
    vals = sb("r_vals", [P, C])
    idx = sb("r_idx", [P, C], U32)
    idxf = sb("r_idxf", [P, C])
    off = sb("r_off", [P, 1])
    vT, iT = sb("r_vT", [P, P]), sb("r_iT", [P, P])
    vB, iB = sb("r_vB", [P, E]), sb("r_iB", [P, E])
    ge, dif, best = sb("r_ge", [P, E]), sb("r_dif", [P, E]), sb("r_best", [P, E])
    pick = sb("r_pick", [P, E])
    rows, mx, ex, sm, rs = (sb("r_rows", [E, C]), sb("r_mx", [E, 1]), sb("r_ex", [E, C]), sb("r_sm", [E, 1]),
                            sb("r_rs", [E, 1]))
    ps = m.ps
    lane = m.lane("r_l")
    t_in = m.sp.dma(lane, Wr[:, :], d["Wr"])
    z = m.memset(m.dve, WrT[:, :], 0.0)
    t = m.transpose(ps[0][:, 0, 0:E], Wr[:, :], k["ident"][0:E, 0:E], t_in)
    w = m.copy(m.dve, WrT[:, 0:E], ps[0][:, 0, 0:E], t, z)
    m.memset(m.dve, off[0:64, :], 0.0)
    t_off = m.memset(m.dve, off[64:P, :], float(HALF))
    x1T_ready, free = [], [w, None]
    for q in range(T // 512):
        bank = ps[0][:, q % 2, :]
        for n in range(4):
            t = m.transpose(bank[:, n * P:(n + 1) * P], x1[:, 4 * q + n, :], k["ident"][:, :], free[q % 2],
                            signal=n == 3)
        free[q % 2] = m.copy(m.dve, x1T[:, q * 512:(q + 1) * 512], bank, t)
        x1T_ready.append(free[q % 2])
    for c in range(HALF // 512):
        out = ps[1 + c // 2][:, c % 2, :]
        m.matmul(out[0:64, :], WrT[:, :], x1T[:, c * 512:(c + 1) * 512], w, x1T_ready[-1])
        t = m.matmul(out[64:P, :], WrT[:, :], x1T[:, HALF + c * 512:HALF + (c + 1) * 512])
        last = m.copy(m.dve, L[:, c * 512:(c + 1) * 512], out, t)
    for r in range(C // 8):
        eight = slice(8 * r, 8 * r + 8)
        t = m.dve.do(lambda e, s=eight: e.max(vals[:, s], L[:, :]), last)
        t = m.dve.do(lambda e, s=eight: e.max_index(idx[:, s], vals[:, s], L[:, :]), t)
        last = m.dve.do(lambda e, s=eight: e.match_replace(L[:, :], vals[:, s], L[:, :], -3.0e38), t)
    t = m.copy(m.dve, idxf[:, :], idx[:, :], last)
    t = m.scalar_op(m.dve, idxf[:, :], idxf[:, :], off[:, 0:1], None, ALU.add, None, t, t_off)
    m.transpose(ps[0][:, 0, 0:P], vals[:, :], k["ident"][:, :], t)
    t = m.transpose(ps[0][:, 0, P:2 * P], idxf[:, :], k["ident"][:, :])
    m.copy(m.dve, vT[:, :], ps[0][:, 0, 0:P], t)
    t = m.copy(m.dve, iT[:, :], ps[0][:, 0, P:2 * P])
    m.matmul(ps[3][:, 0, 0:E], k["mirror"][:, :], vT[:, 64:64 + E], t)
    t = m.matmul(ps[3][:, 0, 64:64 + E], k["mirror"][:, :], iT[:, 64:64 + E])
    m.copy(m.dve, vB[:, :], ps[3][:, 0, 0:E], t)
    t = m.copy(m.dve, iB[:, :], ps[3][:, 0, 64:64 + E])
    m.tensor_op(m.dve, ge[:, :], vT[:, 0:E], vB[:, :], ALU.is_ge, t)
    m.tensor_op(m.dve, best[:, :], vT[:, 0:E], vB[:, :], ALU.max)
    t = m.tensor_op(m.dve, dif[:, :], iT[:, 0:E], iB[:, :], ALU.subtract)
    t = m.tensor_op(m.dve, dif[:, :], dif[:, :], ge[:, :], ALU.mult, t)
    t = m.tensor_op(m.dve, pick[:, :], dif[:, :], iB[:, :], ALU.add, t)
    m.routed = m.copy(m.dve, m.token[:, :], pick[:, :], t)
    t = m.transpose(ps[0][0:E, 1, 0:C], best[:, :], k["ident"][:, :], m.routed)
    a = m.copy(m.dve, rows[:, :], ps[0][0:E, 1, 0:C], t)
    t = m.dve.do(lambda e: e.tensor_reduce(mx[:, :], rows[:, :], AX_X, ALU.max), a)
    t = m.scalar_op(m.dve, rows[:, :], rows[:, :], mx[:, 0:1], None, ALU.subtract, None, t)
    t = m.activate(ex[:, :], rows[:, :], ACT.Exp, t, bias=k["eps"][0:E, 2:3], accum_out=sm[:, 0:1])
    t = m.dve.do(lambda e: e.reciprocal(rs[:, :], sm[:, :]), t)
    t = m.scalar_op(m.dve, ex[:, :], ex[:, :], rs[:, 0:1], None, ALU.mult, None, t)
    t = m.transpose(ps[3][:, 1, 0:E], ex[:, :], k["ident"][0:E, 0:E], t)
    m.share_ready = m.copy(m.dve, m.share[:, :], ps[3][:, 1, 0:E], t)


NACC = 4


def experts(m, d):
    E, NS, D, M = d["W1"].shape
    K = d["W2"].shape[3]
    k, sb = m.k, m.stage_sb
    NB = 4
    xg = sb("e_xg", [P, NB, D])
    xgT = sb("e_xgT", [P, NB, P])
    W1 = sb("e_W1", [P, NB, NS, M])
    W2 = sb("e_W2", [P, NB, NS, K])
    b2 = sb("e_b2", [1, NB, NS * K])
    b1r = sb("e_b1r", [P, 2, M])
    b1T = sb("e_b1T", [P, E * NS])
    hT = sb("e_hT", [P, NB, NS, P])
    y = sb("e_y", [P, NACC, NS * K])
    l_b1 = m.lane("e_l_b1")
    l_w = [m.lane(f"e_l_w{i}") for i in range(NB)]
    l_g = [m.lane(f"e_l_g{i}") for i in range(NB)]
    l_s = [m.lane(f"e_l_s{i}") for i in range(NACC)]
    half = E * NS // 2
    t_b1 = m.sp.dma(l_b1, b1r[0:half, :, :], d["b1"].rearrange("e s m -> (e s) m").rearrange("(a r) m -> r a m", a=2))
    for a in range(2):
        t = m.transpose(m.ps[0][:, 0, a * half:(a + 1) * half], b1r[0:half, a, :], k["ident"][0:half, 0:half], t_b1)
    t_b1T = m.copy(m.dve, b1T[:, :], m.ps[0][:, 0, 0:E * NS], t)
    t_w, t_g = {}, {}
    xg_used, w_used, y_sent = {}, {}, {}

    def load(e):
        i = e % NB
        m.sp.wait(w_used.get(e - NB))
        m.sp.dma(l_w[i], W1[:, i, :, :], d["W1"][e].rearrange("s d m -> d s m"))
        m.sp.dma(l_w[i], W2[:, i, :, :], d["W2"][e].rearrange("s m k -> m s k"))
        t_w[e] = m.sp.dma(l_w[i], b2[:, i, :], d["b2"][e].rearrange("(a s) k -> a (s k)", a=1))
        m.pool.wait(m.routed, *m.x1_stored, xg_used.get(e - NB))
        lane = l_g[i]
        lane.total += 16
        m.pool.queue.append(lambda g, e=e, i=i, lane=lane: g.indirect_dma_start(
            xg[:, i, :], None, m.x1_dram[:, :], bass.IndirectOffsetOnAxis(m.token[:, e:e + 1], 0)).then_inc(lane.sem, 16))
        t_g[e] = (lane.sem, lane.total)

    evac = {}
    ps_free = {}

    def transpose_in(e):
        i = e % NB
        bank = m.ps[0][:, e % 2, 0:P]
        t = m.transpose(bank, xg[:, i, :], k["ident"][:, :], t_g[e], ps_free.get(("x", e % 2)), t_b1T)
        xg_used[e] = t
        v = m.copy(m.dve, xgT[:, i, :], bank, t, w_used.get(e - NB))
        ps_free["x", e % 2] = v
        evac[e] = v

    def hidden(e):
        i = e % NB
        bank = m.ps[1][:, e % 2, :]
        for s in range(NS):
            t = m.matmul(bank[:, s * P:(s + 1) * P], W1[:, i, s, :], xgT[:, i, :], t_w[e], evac[e],
                         ps_free.get(("h", e % 2)), signal=s == NS - 1)
        for s in range(NS):
            a = m.activate(hT[:, i, s, :], bank[:, s * P:(s + 1) * P], ACT.Gelu, t, t_b1T, w_used.get(e - NB),
                           bias=b1T[:, e * NS + s:e * NS + s + 1])
        ps_free["h", e % 2] = a
        return a

    def output(e, a):
        i, j = e % NB, e % NACC
        bank = m.ps[2][:, e % 2, 0:NS * K]
        t = m.matmul(bank, k["ones"][0:1, :], b2[:, i, :], t_w[e], ps_free.get(("y", e % 2)), start=True, stop=False,
                     signal=False)
        for s in range(NS):
            t = m.matmul(bank[:, s * K:(s + 1) * K], hT[:, i, s, :], W2[:, i, s, :], a, start=False, stop=s == NS - 1,
                         signal=s == NS - 1)
        w_used[e] = t
        v = m.scalar_op(m.dve, y[:, j, :], bank, m.share[:, e:e + 1], None, ALU.mult, None, t, m.share_ready,
                        y_sent.get(e - NACC))
        ps_free["y", e % 2] = v
        lane = l_s[j]
        m.pool.wait(v, y_sent.get(e - NACC), *m.x1_stored, m.zeroed)
        lane.total += 16
        m.pool.queue.append(lambda g, e=e, j=j, lane=lane: g.indirect_dma_start(
            m.acc_dram[j][:, :], bass.IndirectOffsetOnAxis(m.token[:, e:e + 1], 0), y[:, j, :], None,
            compute_op=ALU.add).then_inc(lane.sem, 16))
        y_sent[e] = (lane.sem, lane.total)

    act_done = {}
    for e in range(NB - 1):
        load(e)
    for e in range(E + 1):
        if e < E:
            transpose_in(e)
            act_done[e] = hidden(e)
        if e > 0:
            output(e - 1, act_done[e - 1])
        if e + NB - 1 < E:
            load(e + NB - 1)
    m.scattered = [y_sent[e] for e in range(E - NACC, E)]


def join_experts(m, x2):
    NTT = x2.shape[1]
    NT = 4
    sb = m.stage_sb
    A = sb("j_A", [P, 2, NACC, NT, P])
    tmp = ln_buffers(sb, "j_ln", NT)
    lanes = [m.lane(f"j_l{i}") for i in range(2)]
    used = {}
    t_in = {}

    def load(b):
        m.sp.wait(*m.scattered, used.get(b - 2))
        for j in range(NACC):
            t_in[b] = m.sp.dma(lanes[b % 2], A[:, b % 2, j, :, :],
                               m.acc_dram[j][b * NT * P:(b + 1) * NT * P, :].rearrange("(n p) d -> p n d", p=P))

    NBATCH = NTT // NT
    load(0)
    load(1)
    for b in range(NBATCH):
        a = A[:, b % 2]
        m.tensor_op(m.dve, a[:, 0], a[:, 0], a[:, 1], ALU.add, t_in[b])
        t = m.tensor_op(m.pool, a[:, 2], a[:, 2], a[:, 3], ALU.add, t_in[b])
        m.dve.wait((m.dve.sem, m.dve.count))
        t = m.tensor_op(m.dve, a[:, 0], a[:, 0], a[:, 2], ALU.add, t)
        used[b] = m.x2_ready = layernorm_rows(m, a[:, 0], x2[:, b * NT:(b + 1) * NT, :], tmp, NT, t)
        if b + 2 < NBATCH:
            load(b + 2)


def relative_attention(m, d, x2, x3):
    B, T, D, H = 8, 512, 128, 16
    DH = D // H
    G = 4
    NG = H // G
    NT = T // P
    SCALE = float(DH) ** -0.5
    k, sb = m.k, m.stage_sb
    wraw = sb("c_wraw", [P, 3, D])
    wsp = sb("c_wsp", [P, 3, NG, G, 32])
    Wv, Wo = sb("c_Wv", [P, D]), sb("c_Wo", [P, D])
    rows = sb("c_rows", [1, 6, D])
    rsp = sb("c_rsp", [1, 4, NG, G, 32])
    cols = sb("c_cols", [P, 3, NG])
    gb = sb("c_gb", [P, 2])
    bv, bo = sb("c_bv", [P, D]), sb("c_bo", [P, D])
    peT = sb("c_peT", [P, T])
    pT = sb("c_pT", [P, NG, T])
    XN = sb("c_XN", [P, NT, D])
    XNT = sb("c_XNT", [P, T])
    QU, QV, KT = (sb(n, [P, 2, NG, T]) for n in ("c_QU", "c_QV", "c_KT"))
    V = sb("c_V", [P, 2, NT, H, DH + 1])
    NU = 3
    U = sb("c_U", [P, NU, NT, T + 1])
    SK = sb("c_SK", [P, NU, NT, T])
    TS = sb("c_TS", [P, 2, NT, T])
    MX = sb("c_MX", [P, 2, NT])
    EX = sb("c_EX", [P, 2, NT, T])
    RS = sb("c_RS", [P, G, NT])
    HD = sb("c_HD", [P, NT, H, DH])
    HDT = sb("c_HDT", [P, T])
    Y = sb("c_Y", [P, NT, D])
    tmp = ln_buffers(sb, "c_ln", NT)
    tmp2 = ln_buffers(sb, "c_ln2", NT)
    u_ps = [m.ps[0][:, 0, :], m.ps[0][:, 1, :]]
    c_ps = [m.ps[1][:, 0, :], m.ps[1][:, 1, :]]
    t_ps = m.ps[2]
    o_ps, j_ps = m.ps[3][:, 0, :], m.ps[3][:, 1, :]
    o_view = o_ps[:, 0:G * NT * (DH + 1)].rearrange("p (g n c) -> p g n c", g=G, n=NT)

    l_in = m.lane("c_l_in")
    for n, name in enumerate(("Wq", "Wk", "Wp")):
        m.sp.dma(l_in, wraw[:, n, :], d[name])
    m.sp.dma(l_in, Wv[:, :], d["Wv"])
    m.sp.dma(l_in, Wo[:, :], d["Wo"])
    for n, name in enumerate(("bq", "bk", None, None, "ln_g", "ln_b")):
        if name:
            m.sp.dma(l_in, rows[:, n, :], d[name].rearrange("(a e) -> a e", a=1))
    m.sp.dma(l_in, rows[:, 2, :], d["u_bias"].rearrange("(a h) e -> a (h e)", a=1))
    m.sp.dma(l_in, rows[:, 3, :], d["v_bias"].rearrange("(a h) e -> a (h e)", a=1))
    m.sp.dma(l_in, bv[:, :], d["bv"].rearrange("(a e) -> a e", a=1).broadcast_to([P, D]))
    m.sp.dma(l_in, bo[:, :], d["bo"].rearrange("(a e) -> a e", a=1).broadcast_to([P, D]))
    t_in = m.sp.dma(l_in, peT[:, :], d["peT"])

    z1 = m.memset(m.pool, wsp[:, :, :, :, :], 0.0)
    m.memset(m.pool, rsp[:, :, :, :, :], 0.0)
    m.memset(m.pool, V[:, :, :, :, DH:DH + 1], 1.0)
    z2 = m.memset(m.pool, U[:, :, :, 0:1], 0.0)
    for n in range(3):
        t = m.copy(m.dve, wsp[:, n, :, :, 0:DH], wraw[:, n, :].rearrange("p (g r e) -> p g r e", g=NG, r=G),
                   z1, t_in)

    def padded(n):
        return rsp[:, n, :, :, 0:DH]

    def row(n):
        return rows[:, n, :].rearrange("a (g r e) -> a g r e", g=NG, r=G)

    m.tensor_op(m.dve, padded(0), row(0), row(2), ALU.add, z2, t_in)
    m.tensor_op(m.dve, padded(1), row(0), row(3), ALU.add)
    t = m.copy(m.dve, padded(2), row(1))
    for n in range(3):
        for g in range(NG):
            c = m.matmul(j_ps[:, n * NG + g:n * NG + g + 1], rsp[:, n, g, :, :], k["ones"][0:1, 0:1], t)
    for n in range(2):
        c = m.matmul(j_ps[:, 3 * NG + n:3 * NG + n + 1], rows[:, 4 + n, :], k["ones"][0:1, 0:1])
    m.copy(m.dve, cols[:, :, :], j_ps[:, 0:3 * NG].rearrange("p (n g) -> p n g", n=3), c)
    j_free = m.copy(m.dve, gb[:, :], j_ps[:, 3 * NG:3 * NG + 2])
    st = {"j": j_free, "t": [None, None], "u": [None, None], "c": [None, None], "o": None}
    for g in range(NG):
        t = m.matmul(j_ps, wsp[:, 2, g, :, :], peT[:, :], st["j"])
        st["j"] = pT_ready = m.copy(m.dve, pT[:, g, :], j_ps, t)

    l_store = [m.lane(f"c_l_store{i}") for i in range(NU)]
    l_fetch = [m.lane(f"c_l_fetch{i}") for i in range(NU)]
    stored, fetched, sk_used = {}, {}, {}
    ts_ready, ts_used, ex_ready, pv_done, hd_used = {}, {}, {}, {}, [None]
    users = {}
    ready = {}

    def prepare(b):
        s = b % 2
        used = [users.get((b - 2, kind)) for kind in ("pos", "content", "pv")]
        x = x2[:, b * NT:(b + 1) * NT, :]
        r = layernorm_rows(m, x, XN, tmp, NT, m.x2_ready, st.get("xn"))
        for n in range(NT):
            t = m.transpose(j_ps[:, n * P:(n + 1) * P], XN[:, n, :], k["ident"][:, :], r, st["j"], signal=n == NT - 1)
        st["xn"] = t
        st["j"] = xt = m.scalar_op(m.dve, XNT[:, :], j_ps, gb[:, 0:1], gb[:, 1:2], ALU.mult, ALU.add, t, j_free,
                                   st.get("xnt"))
        for g in range(NG):
            t = m.matmul(j_ps, wsp[:, 0, g, :, :], XNT[:, :], xt, st["j"])
            m.scalar_op(m.dve, QU[:, s, g, :], j_ps, cols[:, 0, g:g + 1], None, ALU.add, None, t, *used)
            st["j"] = m.scalar_op(m.dve, QV[:, s, g, :], j_ps, cols[:, 1, g:g + 1], None, ALU.add, None)
            t = m.matmul(j_ps, wsp[:, 1, g, :, :], XNT[:, :], st["j"])
            st["j"] = m.scalar_op(m.dve, KT[:, s, g, :], j_ps, cols[:, 2, g:g + 1], None, ALU.add, None, t)
        for n in range(NT):
            t = m.matmul(j_ps[:, n * P:(n + 1) * P], XNT[:, n * P:(n + 1) * P], Wv[:, :], st["j"])
        st["xnt"] = t
        for n in range(NT):
            v = m.tensor_op(m.dve, V[:, s, n, :, 0:DH], j_ps[:, n * P:(n + 1) * P].rearrange("p (h e) -> p h e", h=H),
                            bv[:, :].rearrange("p (h e) -> p h e", h=H), ALU.add, t)
        st["j"] = v
        ready[b] = v

    def positions(w):
        b, h = divmod(w, H)
        g, r = divmod(h, G)
        i = w % NU
        rs = slice(32 * r, 32 * r + DH)
        for n in range(NT):
            j = n % 2
            t = m.matmul(u_ps[j], QV[rs, b % 2, g, n * P:(n + 1) * P], pT[rs, g, :], ready[b], pT_ready, st["u"][j])
            a = st["u"][j] = m.activate(U[:, i, n, 1:T + 1], u_ps[j], ACT.Copy, t, z2, stored.get(w - NU))
        users[b, "pos"] = t
        stored[w] = m.sp.dma(l_store[i], m.shift_dram[i].rearrange("(n p) c -> p n c", p=P), U[:, i, :, :], a,
                             fetched.get(w - NU))
        flat = m.shift_dram[i].rearrange("a c -> (a c)")[T:T + T * T]
        fetched[w] = m.sp.dma(l_fetch[i], SK[:, i, :, :], flat.rearrange("(n p c) -> p n c", p=P, c=T), stored[w],
                              sk_used.get(w - NU))

    def scores(w):
        b, h = divmod(w, H)
        g, r = divmod(h, G)
        i, s = w % NU, w % 2
        rs = slice(32 * r, 32 * r + DH)
        for n in range(NT):
            j = n % 2
            t = m.matmul(c_ps[j], QU[rs, b % 2, g, n * P:(n + 1) * P], KT[rs, b % 2, g, :], st["c"][j])
            m.dve.wait(t, fetched[w], ts_used.get(w - 2))
            v = st["c"][j] = m.dve.do(lambda e, n=n, j=j: e.tensor_tensor_reduce(
                TS[:, s, n, :], c_ps[j], SK[:, i, n, :], 1.0, -3.0e38, ALU.add, ALU.max, MX[:, s, n:n + 1]))
            p = m.scalar_op(m.pool, TS[:, s, n, :], TS[:, s, n, :], MX[:, s, n:n + 1], None, ALU.subtract, None, v)
        users[b, "content"] = t
        sk_used[w] = v
        ts_ready[w] = p

    def turn_exp(w):
        s = w % 2
        for half in range(2):
            for c in range(2):
                jb = 2 * half + c
                for n in range(NT):
                    t = m.transpose(t_ps[:, c, n * P:(n + 1) * P], TS[:, s, n, jb * P:(jb + 1) * P], k["ident"][:, :],
                                    ts_ready[w], st["t"][0], signal=n == NT - 1)
            a = m.activate(EX[:, s, 2 * half:2 * half + 2, :], t_ps[:, :, :], ACT.Exp, t, pv_done.get(w - 2),
                           scale=SCALE, bias=k["eps"][:, 2:3])
            st["t"][0] = a
        ts_used[w] = t
        ex_ready[w] = a

    def apply(w):
        b, h = divmod(w, H)
        g, r = divmod(h, G)
        s = w % 2
        for n in range(NT):
            for jb in range(NT):
                t = m.matmul(o_view[:, r, n, :], EX[:, s, jb, n * P:(n + 1) * P], V[:, b % 2, jb, h, :], ex_ready[w],
                             st["o"], start=jb == 0, stop=jb == NT - 1, signal=jb == NT - 1)
        pv_done[w] = users[b, "pv"] = t
        if r == G - 1:
            v = m.dve.do(lambda e: e.reciprocal(RS[:, :, :], o_view[:, :, :, DH]), t)
            for n in range(NT):
                v = m.tensor_op(m.dve, HD[:, n, g * G:(g + 1) * G, :], o_view[:, :, n, 0:DH],
                                RS[:, :, n:n + 1].broadcast_to([P, G, DH]), ALU.mult, v, hd_used[0])
            st["o"] = v
            if g == NG - 1:
                finish(b, v)

    def finish(b, hd_ready):
        x = x2[:, b * NT:(b + 1) * NT, :]
        for n in range(NT):
            xb = m.tensor_op(m.pool, Y[:, n, :], x[:, n, :], bo[:, :], ALU.add, m.x2_ready, t_in, st.get("y"))
            t = m.transpose(j_ps[:, n * P:(n + 1) * P], HD[:, n, :, :].rearrange("p h e -> p (h e)"),
                            k["ident"][:, :], hd_ready, st["j"], signal=n == NT - 1)
        hd_used[0] = t
        st["j"] = v = m.copy(m.dve, HDT[:, :], j_ps, t, st.get("hdt"))
        for n in range(NT):
            t = m.matmul(j_ps[:, n * P:(n + 1) * P], HDT[:, n * P:(n + 1) * P], Wo[:, :], v)
        st["hdt"] = t
        st["j"] = v = m.tensor_op(m.dve, Y[:, :, :], j_ps.rearrange("p (n c) -> p n c", n=NT), Y[:, :, :],
                                  ALU.add, t, xb)
        m.x3_ready = st["y"] = layernorm_rows(m, Y, x3[:, b * NT:(b + 1) * NT, :], tmp2, NT, v)

    W = B * H
    LEAD = 2
    prepare(0)
    for step in range(W + LEAD + 1):
        if step < W:
            positions(step)
        if 0 <= step - LEAD < W:
            scores(step - LEAD)
        if 0 <= step - LEAD - 1 < W:
            turn_exp(step - LEAD - 1)
            apply(step - LEAD - 1)
        if step % H == H - 4 and step // H + 1 < B:
            prepare(step // H + 1)


def gated_ffn(m, d, x3, out):
    NTT = x3.shape[1]
    D, E = d["gate_w"].shape
    NT = 4
    k, sb = m.k, m.stage_sb
    raw = sb("f_raw", [P, 2, D])
    WT = sb("f_WT", [P, 2 * D + E])
    bb = sb("f_bb", [P, 2 * D])
    XT = sb("f_XT", [P, NTT, P])
    PRE = sb("f_PRE", [P, NTT, 2 * D])
    LG = sb("f_LG", [P, NTT, E])
    red = sb("f_red", [P, NTT])
    inv = sb("f_inv", [P, NTT])
    cmp = sb("f_cmp", [P, NTT, E])
    rank, m0, m1 = sb("f_rank", [P, NTT]), sb("f_m0", [P, NTT]), sb("f_m1", [P, NTT])
    coef = sb("f_coef", [P, 2, NTT])
    Y = sb("f_Y", [P, NTT, D])
    O = sb("f_O", [P, NTT, D])
    tmp = ln_buffers(sb, "f_ln", NTT)
    lane, l_out = m.lane("f_l"), m.lane("f_l_out")
    m.sp.dma(lane, raw[:, 0, :], d["w0"])
    m.sp.dma(lane, raw[:, 1, :], d["w1"])
    m.sp.dma(lane, WT[:, 2 * D:2 * D + E], d["gate_w"])
    m.sp.dma(lane, bb[:, 0:D], d["b0"].rearrange("(a e) -> a e", a=1).broadcast_to([P, D]))
    t_in = m.sp.dma(lane, bb[:, D:2 * D], d["b1"].rearrange("(a e) -> a e", a=1).broadcast_to([P, D]))
    for n in range(2):
        t = m.transpose(m.ps[0][:, 0, n * P:(n + 1) * P], raw[:, n, :], k["ident"][:, :], t_in)
    w = m.copy(m.dve, WT[:, 0:2 * D], m.ps[0][:, 0, 0:2 * D], t)
    free = {"x0": w, "x1": None, "m0": None, "m1": None}
    for q in range(NTT // NT):
        key = f"x{q % 2}"
        bank = m.ps[0][:, q % 2, :]
        for n in range(NT):
            t = m.transpose(bank[:, n * P:(n + 1) * P], x3[:, q * NT + n, :], k["ident"][:, :], free[key],
                            signal=n == NT - 1)
        free[key] = xt = m.copy(m.dve, XT[:, q * NT:(q + 1) * NT, :], bank.rearrange("p (n c) -> p n c", n=NT), t)
        for n in range(NT):
            i = q * NT + n
            key2 = f"m{n % 2}"
            ps = m.ps[1][:, n % 2, 0:2 * D + E]
            t = m.matmul(ps, XT[:, i, :], WT[:, :], xt, w, free[key2])
            m.copy(m.dve, LG[:, i, :], ps[:, 2 * D:2 * D + E], t)
            free[key2] = pre = m.tensor_op(m.dve, PRE[:, i, :], ps[:, 0:2 * D], bb[:, :], ALU.add)

    def over_experts(col):
        return col.unsqueeze(2).broadcast_to([P, NTT, E])

    t = m.dve.do(lambda e: e.tensor_reduce(red[:, :], LG[:, :, :], AX_X, ALU.max), pre)
    t = m.tensor_op(m.dve, LG[:, :, :], LG[:, :, :], over_experts(red[:, :]), ALU.subtract, t)
    t = m.activate(LG[:, :, :], LG[:, :, :], ACT.Exp, t, bias=k["eps"][:, 2:3])
    t = m.dve.do(lambda e: e.tensor_reduce(red[:, :], LG[:, :, :], AX_X, ALU.add), t)
    t = m.dve.do(lambda e: e.reciprocal(inv[:, :], red[:, :]), t)
    t = m.tensor_op(m.dve, LG[:, :, :], LG[:, :, :], over_experts(inv[:, :]), ALU.mult, t)
    t = m.dve.do(lambda e: e.tensor_reduce(red[:, :], LG[:, :, 1:E], AX_X, ALU.max), t)
    t = m.tensor_op(m.dve, m0[:, :], LG[:, :, 0], red[:, :], ALU.is_ge, t)
    m.tensor_op(m.dve, coef[:, 0, :], LG[:, :, 0], m0[:, :], ALU.mult, t)
    m.tensor_op(m.dve, cmp[:, :, 2:E], LG[:, :, 2:E], LG[:, :, 1:2].broadcast_to([P, NTT, E - 2]), ALU.is_gt)
    t = m.tensor_op(m.dve, cmp[:, :, 1], LG[:, :, 0], LG[:, :, 1], ALU.is_ge)
    t = m.dve.do(lambda e: e.tensor_reduce(rank[:, :], cmp[:, :, 1:E], AX_X, ALU.add), t)
    t = m.scalar_op(m.dve, m1[:, :], rank[:, :], 1.0, None, ALU.is_equal, None, t)
    c = m.tensor_op(m.dve, coef[:, 1, :], LG[:, :, 1], m1[:, :], ALU.mult, t)
    for q in range(NTT // NT):
        tiles = slice(q * NT, (q + 1) * NT)
        a = m.activate(PRE[:, tiles, :], PRE[:, tiles, :], ACT.Silu, pre)
        for i in range(q * NT, (q + 1) * NT):
            t = m.scalar_op(m.dve, Y[:, i, :], PRE[:, i, 0:D], coef[:, 0, i:i + 1], None, ALU.mult, None, a, c)
            m.dve.wait(t)
            t = m.dve.do(lambda e, i=i: e.scalar_tensor_tensor(Y[:, i, :], PRE[:, i, D:2 * D], coef[:, 1, i:i + 1],
                                                              Y[:, i, :], ALU.mult, ALU.add))
        t = m.tensor_op(m.dve, Y[:, tiles, :], Y[:, tiles, :], x3[:, tiles, :], ALU.add, t)
    r = layernorm_rows(m, Y, O, tmp, NTT, t)
    t = m.sp.dma(l_out, out.rearrange("b (n p) d -> p (b n) d", p=P), O[:, :, :], r)
    m.sp.wait(t)


def two_layers_kernel(nc, ins, out):
    B, T, D = ins["L0_attn_X"].shape
    rows = B * T
    NTT = rows // P

    def part(prefix):
        return {n[len(prefix):]: ap for n, ap in ins.items() if n.startswith(prefix)}

    with ExitStack() as ctx:
        m = Machine(nc, ctx)
        m.ps = [ctx.enter_context(nc.psum_tensor(f"ps{i}", [P, 2, 512], F32)) for i in range(4)]
        m.x1_dram = nc.dram_tensor("x1_dram", (rows, D), F32, kind="Internal").ap()
        m.acc_dram = [nc.dram_tensor(f"acc_dram{j}", (rows, D), F32, kind="Internal").ap() for j in range(NACC)]
        m.shift_dram = [nc.dram_tensor(f"shift_dram{j}", (T, T + 1), F32, kind="Internal").ap() for j in range(3)]
        make_constants(m)
        xA = m.sb("x_a", [P, NTT, D])
        m.token = m.sb("token", [P, 48], U32)
        m.share = m.sb("share", [P, 48])

        with ExitStack() as x1_ctx:
            zeros = x1_ctx.enter_context(nc.sbuf_tensor("zeros", [P, 4 * D], F32))
            z = m.memset(m.pool, zeros[:, :], 0.0)
            l_zero = m.lane("l_zero")
            for j in range(1, NACC):
                for q in range(NTT // 4):
                    m.zeroed = m.sp.dma(l_zero, m.acc_dram[j][q * 4 * P:(q + 1) * 4 * P, :]
                                        .rearrange("(p n) d -> p (n d)", p=P), zeros[:, :], z)
            with ExitStack() as m.stage_ctx:
                m.stage("dist")
                distance_attention(m, part("L0_attn_"), xA)
                m.close_stage()
            with ExitStack() as m.stage_ctx:
                m.stage("route")
                route(m, part("L0_ffn_"), xA)
                m.close_stage()
            with ExitStack() as m.stage_ctx:
                m.stage("experts")
                experts(m, part("L0_ffn_"))
                m.close_stage()
        xB = m.sb("x_b", [P, NTT, D])
        with ExitStack() as m.stage_ctx:
            m.stage("join")
            join_experts(m, xA)
            m.close_stage()
        with ExitStack() as m.stage_ctx:
            m.stage("rel")
            relative_attention(m, dict(part("L1_attn_"), peT=ins["peT"]), xA, xB)
            m.close_stage()
        with ExitStack() as m.stage_ctx:
            m.stage("ffn")
            gated_ffn(m, part("L1_ffn_"), xB, out)

        with nc.Block() as block:
            block.sync(lambda e: m.sp.play(e))
            block.gpsimd(lambda e: m.pool.play(e))
            block.scalar(lambda e: m.act.play(e))
            block.vector(lambda e: m.dve.play(e))
            block.tensor(lambda e: m.pe.play(e))


_INS = ["L0_attn_X", "L0_attn_W_in", "L0_attn_b_in", "L0_attn_W_out", "L0_attn_b_out", "L0_ffn_Wr", "L0_ffn_W1",
        "L0_ffn_b1", "L0_ffn_W2", "L0_ffn_b2", "L1_attn_ln_g", "L1_attn_ln_b", "L1_attn_Wq", "L1_attn_bq",
        "L1_attn_Wk", "L1_attn_bk", "L1_attn_Wv", "L1_attn_bv", "L1_attn_Wp", "L1_attn_Wo", "L1_attn_bo",
        "L1_attn_u_bias", "L1_attn_v_bias", "L1_ffn_gate_w", "L1_ffn_w0", "L1_ffn_b0", "L1_ffn_w1", "L1_ffn_b1"]


def position_table(length, width):
    pos = np.arange(length, dtype=np.float32)[:, None]
    div = np.exp(np.arange(0, width, 2, dtype=np.float32) * np.float32(-np.log(10000.0) / width)).astype(np.float32)
    ang = (pos * div).astype(np.float32)
    pe = np.stack([np.sin(ang), np.cos(ang)], axis=-1).reshape(length, width).astype(np.float32)
    return np.ascontiguousarray(pe.T)


def kernel(**inputs):
    import concourse.bacc as _bacc
    from concourse.bass_utils import run_bass_kernel_spmd as _run

    nc = _bacc.Bacc("TRN2", target_bir_lowering=False, num_devices=1)
    arrays, args = {}, {}
    for name in _INS:
        a = np.ascontiguousarray(inputs[name])
        arrays[f"in_{name}"] = a
        args[name] = nc.dram_tensor(f"in_{name}", a.shape, mybir.dt.from_np(a.dtype), kind="ExternalInput").ap()
    shape = tuple(inputs["L0_attn_X"].shape)
    peT = position_table(shape[1], shape[2])
    arrays["in_peT"] = peT
    args["peT"] = nc.dram_tensor("in_peT", peT.shape, F32, kind="ExternalInput").ap()
    out = nc.dram_tensor("out", shape, F32, kind="ExternalOutput").ap()
    two_layers_kernel(nc, args, out)
    r = _run(nc, [arrays], core_ids=[0])
    return r.results[0]["out"]
```

```python
from contextlib import ExitStack

import numpy as np
import concourse.bass as bass
from concourse import mybir

ALU = mybir.AluOpType
ACT = mybir.ActivationFunctionType
F32 = mybir.dt.float32
U32 = mybir.dt.uint32
AX_X = mybir.AxisListType.X

P = 128
LN_EPS = 1e-5
POW_EPS = 1e-4


class Line:

    def __init__(self, name, new_sem, in_order=False):
        self.name, self.new_sem, self.in_order, self.last = name, new_sem, in_order, None
        self.queue, self.waited = [], {}
        self.stage("start")

    def stage(self, stage):
        self.sem, self.count = self.new_sem(f"{self.name}_{stage}"), 0

    def wait(self, *tickets):
        for t in tickets:
            if t is None:
                continue
            sem, value = t
            if self.waited.get(sem.name, 0) < value:
                self.waited[sem.name] = value
                self.queue.append(lambda e, s=sem, v=value: e.wait_ge(s, v))

    def do(self, emit, *needs, signal=True):
        self.wait(*needs, self.last if self.in_order else None)
        if not signal:
            self.queue.append(emit)
            return None
        self.count += 1
        sem = self.sem
        self.queue.append(lambda e: emit(e).then_inc(sem, 1))
        self.last = (sem, self.count)
        return self.last

    def dma(self, lane, out, in_, *needs):
        self.wait(*needs)
        lane.total += 16
        self.queue.append(lambda e: e.dma_start(out, in_).then_inc(lane.sem, 16))
        return (lane.sem, lane.total)

    def play(self, engine):
        for step in self.queue:
            step(engine)


class Lane:

    def __init__(self, sem):
        self.sem, self.total = sem, 0


class Machine:

    def __init__(self, nc, ctx):
        self.nc, self.ctx = nc, ctx
        self.pe = Line("pe", self.semaphore)
        self.act = Line("act", self.semaphore)
        self.dve = Line("dve", self.semaphore)
        self.pool = Line("pool", self.semaphore, in_order=True)
        self.sp = Line("sp", self.semaphore)
        self.stage_ctx = None

    def semaphore(self, name):
        return self.ctx.enter_context(self.nc.semaphore(name))

    def lane(self, name):
        return Lane(self.semaphore(name))

    def sb(self, name, shape, dt=F32):
        return self.ctx.enter_context(self.nc.sbuf_tensor(name, shape, dt))

    def stage_sb(self, name, shape, dt=F32):
        return self.stage_ctx.enter_context(self.nc.sbuf_tensor(name, shape, dt))

    def stage(self, name):
        for line in (self.pe, self.act, self.dve, self.pool, self.sp):
            line.stage(name)

    def close_stage(self):
        lines = (self.pe, self.act, self.dve, self.pool)
        last = [(line.sem, line.count) for line in lines if line.count]
        for line in lines + (self.sp,):
            line.wait(*[t for t in last if t[0] is not line.sem])
            line.wait(*[t for t in last if t[0] is line.sem])

    def matmul(self, out, lhsT, rhs, *needs, start=True, stop=True, signal=True):
        return self.pe.do(lambda e: e.matmul(out, lhsT, rhs, start=start, stop=stop), *needs, signal=signal)

    def transpose(self, out, in_, ident, *needs, signal=True):
        return self.pe.do(lambda e: e.transpose(out, in_, ident), *needs, signal=signal)

    def activate(self, out, in_, func, *needs, **kw):
        return self.act.do(lambda e: e.activation(out, in_, func, **kw), *needs)

    def load_table(self, name):
        self.act.do(lambda e: e.preload_act_table_set(name), signal=False)

    def scalar_op(self, line, out, in_, s1, s2, op0, op1, *needs):
        if op1 is None:
            return line.do(lambda e: e.tensor_scalar(out, in_, s1, None, op0), *needs)
        return line.do(lambda e: e.tensor_scalar(out, in_, s1, s2, op0, op1), *needs)

    def tensor_op(self, line, out, a, b, op, *needs):
        return line.do(lambda e: e.tensor_tensor(out, a, b, op), *needs)

    def copy(self, line, out, in_, *needs):
        return line.do(lambda e: e.tensor_copy(out, in_), *needs)

    def memset(self, line, out, value, *needs):
        return line.do(lambda e: e.memset(out, value), *needs)


def make_constants(m):
    k = m.k = {}
    k["ident"], k["mirror"], k["ones"] = (m.sb(n, [P, P]) for n in ("ident", "mirror", "ones"))
    k["eps"] = m.sb("eps_cols", [P, 4])
    a = m.memset(m.pool, k["ident"][:, :], 0.0)
    b = m.memset(m.pool, k["mirror"][:, :], 0.0)
    m.pool.wait(a, b)
    m.pool.do(lambda e: e.affine_select(out=k["ident"][:, :], in_=k["ident"][:, :], compare_op=ALU.not_equal,
                                        fill=1.0, base=0, pattern=[[-1, P]], channel_multiplier=1))
    m.pool.do(lambda e: e.affine_select(out=k["mirror"][:, :], in_=k["mirror"][:, :], compare_op=ALU.not_equal,
                                        fill=1.0, base=1 - P, pattern=[[1, P]], channel_multiplier=1))
    m.memset(m.pool, k["ones"][:, :], 1.0)
    m.memset(m.pool, k["eps"][:, 0:1], POW_EPS)
    m.memset(m.pool, k["eps"][:, 1:2], LN_EPS)
    k["ready"] = m.memset(m.pool, k["eps"][:, 2:3], 0.0)


def layernorm_rows(m, x, out, tmp, n, *needs, on=None):
    stats, mv, lg, rstd = tmp
    for i in range(n):
        t = m.dve.do(lambda e, i=i: e.bn_stats(stats[:, i, :], x[:, i, :]), *needs)
        needs = ()
    m.dve.wait(t)
    for i in range(n):
        t = m.dve.do(lambda e, i=i: e.bn_aggr(mv[:, i, :], stats[:, i, :]))
    t1 = m.activate(lg[:, 0:n], mv[:, 0:n, 1], ACT.Ln, t, m.k["ready"], bias=m.k["eps"][:, 1:2])
    t2 = m.activate(rstd[:, 0:n], lg[:, 0:n], ACT.Exp, t1, scale=-0.5, bias=m.k["eps"][:, 2:3])
    for i in range(n):
        r = m.scalar_op(m.dve, out[:, i, :], x[:, i, :], mv[:, i, 0:1], rstd[:, i:i + 1],
                        ALU.subtract, ALU.mult, t2)
    return r


def ln_buffers(make, name, n):
    return (make(name + "_stats", [P, n, 6]), make(name + "_mv", [P, n, 2]),
            make(name + "_lg", [P, n]), make(name + "_rstd", [P, n]))


def distance_attention(m, d, x1):
    B, T, D = d["X"].shape
    H, E = 16, 64
    G = 4
    NG = H // G
    NT = T // P
    sb = m.stage_sb
    k = m.k
    W = sb("a_W_in", [P, 4, H, E])
    Wo = sb("a_W_out", [P, H // 2, D])
    brow = sb("a_b_rows", [4 * H, E])
    bcol = sb("a_b_cols", [P, H // 2, 4])
    bk2 = sb("a_bk_m2", [P, H // 2])
    bv = sb("a_bv", [P, H, E])
    bo = sb("a_bo", [P, D])
    pick = sb("a_pick", [P, 2, G])
    X = sb("a_X", [P, 2, NT, D])
    XT = sb("a_XT", [P, 2, T])
    QA = sb("a_QA", [E + 1, 2, G, T])
    KA = sb("a_KA", [E + 1, 2, G, T])
    GT = sb("a_GT", [P, 2, 2, T])
    V = sb("a_V", [P, 2, NT, G, E])
    SQ = sb("a_SQ", [P, 2, 2, T])
    q2s = sb("a_q2", [G, T])
    k2s = sb("a_k2", [P, 2, NT, G])
    S = sb("a_S", [P, 2, G, NT, T])
    W2 = sb("a_W2", [P, 2, T])
    WS = sb("a_WS", [P, G, T])
    RR = sb("a_RR", [P, T])
    HT = sb("a_HT", [P, H // 2, T])
    Y = sb("a_Y", [P, NT, D])
    tmp = ln_buffers(sb, "a_ln", NT)
    score_ps, pv_ps, prj_ps = m.ps[0:2], m.ps[2], m.ps[3]

    l_w, l_b, l_x = m.lane("a_l_w"), m.lane("a_l_b"), [m.lane(f"a_l_x{i}") for i in range(2)]
    m.sp.dma(l_x[0], X[:, 0, :, :], d["X"][0].rearrange("(n p) d -> p n d", p=P))
    t_x = [(l_x[0].sem, l_x[0].total), None]
    m.sp.dma(l_b, brow[:, :], d["b_in"].rearrange("(r e) -> r e", e=E))
    m.sp.dma(l_b, bv[:, :, :], d["b_in"].rearrange("(a h c e) -> a h c e", a=1, h=H, c=4)[:, :, 2, :]
             .broadcast_to([P, H, E]))
    m.sp.dma(l_b, bo[:, :], d["b_out"].rearrange("(a e) -> a e", a=1).broadcast_to([P, D]))
    t_b = (l_b.sem, l_b.total)
    for c in range(4):
        m.sp.dma(l_w, W[:, c, :, :], d["W_in"].rearrange("p (h c e) -> p h c e", h=H, c=4)[:, :, c, :])
    m.sp.dma(l_w, Wo[:, :, :], d["W_out"].rearrange("(q p) n -> p q n", p=P))
    t_w = (l_w.sem, l_w.total)

    t = m.memset(m.pool, pick[:, :, :], 0.0)
    m.pool.wait(t)
    for pr in range(2):
        for odd in range(2):
            m.memset(m.pool, pick[E * odd:E * odd + E, pr, 2 * pr + odd:2 * pr + odd + 1], 1.0)
    m.memset(m.pool, KA[E:E + 1, :, :, :], 1.0)
    t_const = (m.pool.sem, m.pool.count)

    t = m.transpose(prj_ps[0:E, 0, 0:4 * H], brow[:, :], k["ident"][0:4 * H, 0:4 * H], t_b, k["ready"])
    src = prj_ps[0:E, 0, 0:4 * H].rearrange("p (q o c) -> p o q c", o=2, c=4)
    m.copy(m.dve, bcol[0:E, :, :], src[:, 0], t)
    t = m.copy(m.dve, bcol[E:P, :, :], src[:, 1])
    t_bc = m.scalar_op(m.dve, bk2[:, :], bcol[:, :, 1], -2.0, None, ALU.mult, None, t)

    prj_free = [t_bc, None]
    turn = {"prj": 1, "score": 0}
    score_free = [None, None]
    pv_free = [None, None]
    xT_ready, xT_used = {}, {}
    SQ_used = [None, None]
    q2_lane, q2_sent = m.lane("a_l_q2"), [None]
    S_used = [None, None]
    unit_ready, d2_done, w_done, pv_done = {}, {}, {}, {}
    gt_used = {}
    ht_used = [None]
    x_used = {}
    out_lane = [m.lane("a_l_x1d"), m.lane("a_l_acc")]

    def prj_bank():
        i = turn["prj"]
        turn["prj"] = 1 - i
        return i, prj_ps[:, i, :], prj_free[i]

    def load_x(b):
        if b < B and b > 0:
            t_x[b % 2] = m.sp.dma(l_x[b % 2], X[:, b % 2, :, :], d["X"][b].rearrange("(n p) d -> p n d", p=P),
                                  x_used.get(b - 2))

    def transpose_x(b):
        i, bank, free = prj_bank()
        for n in range(NT):
            t = m.transpose(bank[:, n * P:(n + 1) * P], X[:, b % 2, n, :], k["ident"][:, :], t_x[b % 2], free,
                            k["ready"], signal=n == NT - 1)
        xT_ready[b] = m.copy(m.dve, XT[:, b % 2, :], bank, t, xT_used.get(b - 2))
        prj_free[i] = xT_ready[b]

    def project_pair(u, pr):
        b, g = divmod(u, NG)
        s = u % 2
        q = 2 * g + pr
        before = pv_done.get(u - 2)
        for part in (0, 1, 3):
            i, bank, free = prj_bank()
            t = m.matmul(bank, W[:, part, 2 * q:2 * q + 2, :], XT[:, b % 2, :], t_w, xT_ready[b], free)
            if part == 3:
                last = m.scalar_op(m.dve, GT[:, s, pr, :], bank, bcol[:, q, 3:4], None, ALU.add, None, t, t_bc,
                                   gt_used.get(u - 2))
                prj_free[i] = last
                continue
            a = m.activate(SQ[:, part, pr, :], bank, ACT.Square, t, t_bc, SQ_used[part], bias=bcol[:, q, part:part + 1])
            unit_sq[part][pr] = a
            for odd in range(2):
                rows = slice(E * odd, E * odd + E)
                if part == 0:
                    v = m.scalar_op(m.dve, QA[0:E, s, 2 * pr + odd, :], bank[rows, :], bcol[rows, q, 0:1], None,
                                    ALU.add, None, t, t_bc, before, a)
                else:
                    v = m.scalar_op(m.dve, KA[0:E, s, 2 * pr + odd, :], bank[rows, :], -2.0, bk2[rows, q:q + 1],
                                    ALU.mult, ALU.add, t, t_bc, before, a)
            prj_free[i] = v

    unit_sq = [[None, None], [None, None]]

    def project_rest(u):
        b, g = divmod(u, NG)
        s = u % 2
        before = pv_done.get(u - 2)
        i, bank, free = prj_bank()
        for pr in range(2):
            t = m.matmul(bank[0:G, :], pick[:, pr, :], SQ[:, 0, pr, :], unit_sq[0][pr], t_const, free,
                         start=pr == 0, stop=pr == 1, signal=pr == 1)
        SQ_used[0] = t
        t = m.copy(m.dve, q2s[:, :], bank[0:G, :], t, q2_sent[0])
        prj_free[i] = t
        q2_sent[0] = m.sp.dma(q2_lane, QA[E:E + 1, s, :, :].rearrange("a g t -> a (g t)"), q2s[:, :], t, before)
        i, bank, free = prj_bank()
        for n in range(NT):
            for pr in range(2):
                t = m.matmul(bank[:, G * n + 2 * pr:G * n + 2 * pr + 2], SQ[:, 1, pr, n * P:(n + 1) * P],
                             pick[:, 0, 0:2], unit_sq[1][pr], free, signal=n == NT - 1 and pr == 1)
        SQ_used[1] = t
        k2 = m.copy(m.dve, k2s[:, s, :, :], bank[:, 0:G * NT].rearrange("p (n g) -> p n g", g=G), t, before)
        prj_free[i] = k2
        for half in range(2):
            i, bank, free = prj_bank()
            for n in range(2):
                t = m.matmul(bank[:, n * G * E:(n + 1) * G * E], XT[:, b % 2, (2 * half + n) * P:(2 * half + n + 1) * P],
                             W[:, 2, G * g:G * g + G, :], free, signal=n == 1)
            xT_used[b] = t
            for n in range(2):
                src = bank[:, n * G * E:(n + 1) * G * E].rearrange("p (g e) -> p g e", g=G)
                t = m.tensor_op(m.dve, V[:, s, 2 * half + n, :, :], src, bv[:, G * g:G * g + G, :], ALU.add,
                                t, t_b, before)
            prj_free[i] = t
        unit_ready[u] = (t, q2_sent[0])

    def distances(u, h):
        s = u % 2
        for half in range(2):
            i = turn["score"]
            turn["score"] = 1 - i
            ps = score_ps[i]
            for n in range(2):
                sl = 2 * half + n
                t = m.matmul(ps[:, n, :], KA[:, s, h, sl * P:(sl + 1) * P], QA[:, s, h, :], *unit_ready[u],
                             score_free[i], t_const)
                v = m.scalar_op(m.dve, S[:, s, h, sl, :], ps[:, n, :], k2s[:, s, sl, h:h + 1], 0.0, ALU.add, ALU.max,
                                t, S_used[s])
            score_free[i] = v
        flat = S[:, s, h, :, :].rearrange("p n t -> p (n t)")
        d2_done[u, h] = m.activate(flat, flat, ACT.Sqrt, v, bias=k["eps"][:, 2:3])

    def weights(u, h):
        s = u % 2
        flat = S[:, s, h, :, :].rearrange("p n t -> p (n t)")
        t = m.activate(flat, flat, ACT.Ln, d2_done[u, h], k["ready"], bias=k["eps"][:, 0:1])
        w_done[u, h] = m.activate(flat, flat, ACT.Exp, t, scale=-2.0, bias=k["eps"][:, 2:3])

    def sum_tiles(u, h):
        s = u % 2
        m.tensor_op(m.pool, W2[:, :, :], S[:, s, h, 0:2, :], S[:, s, h, 2:4, :], ALU.add, w_done[u, h])
        ws_done[u, h] = m.tensor_op(m.pool, WS[:, h, :], W2[:, 0, :], W2[:, 1, :], ALU.add, ws_used[h])

    def apply_pair(u, pr):
        b, g = divmod(u, NG)
        s = u % 2
        values, sums = pv_ps[:, 0, :], pv_ps[:, 1, :]
        rows = [slice(0, E), slice(E, P)]
        heads = (2 * pr, 2 * pr + 1)
        for n in range(NT):
            for odd, h in enumerate(heads):
                t = m.matmul(values[rows[odd], :], V[:, s, n, h, :], S[:, s, h, n, :], w_done[u, h], pv_free[0],
                             start=n == 0, stop=n == NT - 1, signal=n == NT - 1)
        pv_done[u] = t
        for odd, h in enumerate(heads):
            c = m.matmul(sums[rows[odd], :], k["ones"][:, 0:E], WS[:, h, :], ws_done[u, h], pv_free[1])
            ws_used[h] = c
        S_used[s] = c
        a = m.activate(RR[:, :], sums, ACT.Ln, c, rr_used[0], bias=k["eps"][:, 0:1])
        pv_free[1] = a
        a = m.activate(RR[:, :], RR[:, :], ACT.Exp, a, scale=-1.0, bias=k["eps"][:, 2:3])
        v = m.tensor_op(m.dve, RR[:, :], RR[:, :], GT[:, s, pr, :], ALU.mult, a)
        gt_used[u] = v
        v = m.tensor_op(m.dve, HT[:, 2 * g + pr, :], values, RR[:, :], ALU.mult, v, t, ht_used[0])
        pv_free[0] = rr_used[0] = ht_ready[0] = v

    rr_used, ht_ready, ws_used, ws_done = [None], [None], [None] * G, {}

    def finish_batch(b):
        t_xb = None
        for n in range(NT):
            t_xb = m.tensor_op(m.pool, Y[:, n, :], X[:, b % 2, n, :], bo[:, :], ALU.add, t_b, t_x[b % 2],
                               y_done[0])
        i, bank, free = prj_bank()
        for n in range(NT):
            for q in range(H // 2):
                t = m.matmul(bank[:, n * P:(n + 1) * P], HT[:, q, n * P:(n + 1) * P], Wo[:, q, :], ht_ready[0], free,
                             start=q == 0, stop=q == H // 2 - 1, signal=q == H // 2 - 1 and n == NT - 1)
        ht_used[0] = t
        x_used[b] = t_xb
        v = m.tensor_op(m.dve, Y[:, :, :], bank.rearrange("p (n c) -> p n c", n=NT), Y[:, :, :], ALU.add, t, t_xb)
        prj_free[i] = v
        load_x(b + 2)
        o = x1[:, b * NT:(b + 1) * NT, :]
        r = y_done[0] = layernorm_rows(m, Y, o, tmp, NT, v)
        rows = slice(b * T, (b + 1) * T)
        m.sp.dma(out_lane[0], m.x1_dram[rows, :].rearrange("(n p) d -> p n d", p=P), o, r)
        m.sp.dma(out_lane[1], m.acc_dram[0][rows, :].rearrange("(n p) d -> p n d", p=P), o, r)

    y_done = [None]

    units = B * NG
    load_x(1)
    transpose_x(0)
    project_pair(0, 0)
    project_pair(0, 1)
    project_rest(0)
    for u in range(units + 1):
        if u > 0:
            for h in range(G):
                sum_tiles(u - 1, h)
        if u < units:
            for h in range(G):
                distances(u, h)
            m.load_table("natural_log_exp_and_others")
            weights(u, 0)
        if u + 1 < units:
            if (u + 1) % NG == 0:
                transpose_x((u + 1) // NG)
        if u > 0:
            apply_pair(u - 1, 0)
        if u + 1 < units:
            project_pair(u + 1, 0)
        if u < units:
            weights(u, 1)
        if u > 0:
            apply_pair(u - 1, 1)
        if u + 1 < units:
            project_pair(u + 1, 1)
        if u < units:
            weights(u, 2)
        if u + 1 < units:
            project_rest(u + 1)
        if u < units:
            weights(u, 3)
        if u > 0 and (u - 1) % NG == NG - 1:
            finish_batch((u - 1) // NG)
    m.x1_stored = [(l.sem, l.total) for l in out_lane]


def route(m, d, x1):
    E, D = d["Wr"].shape
    T = x1.shape[1] * P
    C = int(1.5 * T / E)
    HALF = T // 2
    k, sb = m.k, m.stage_sb
    assert C == P
    x1T = sb("r_x1T", [P, T])
    Wr = sb("r_Wr", [E, D])
    WrT = sb("r_WrT", [P, 64])
    L = sb("r_L", [P, HALF])
    vals = sb("r_vals", [P, C])
    idx = sb("r_idx", [P, C], U32)
    idxf = sb("r_idxf", [P, C])
    off = sb("r_off", [P, 1])
    vT, iT = sb("r_vT", [P, P]), sb("r_iT", [P, P])
    vB, iB = sb("r_vB", [P, E]), sb("r_iB", [P, E])
    ge, dif, best = sb("r_ge", [P, E]), sb("r_dif", [P, E]), sb("r_best", [P, E])
    pick = sb("r_pick", [P, E])
    rows, mx, ex, sm, rs = (sb("r_rows", [E, C]), sb("r_mx", [E, 1]), sb("r_ex", [E, C]), sb("r_sm", [E, 1]),
                            sb("r_rs", [E, 1]))
    ps = m.ps
    lane = m.lane("r_l")
    t_in = m.sp.dma(lane, Wr[:, :], d["Wr"])
    z = m.memset(m.dve, WrT[:, :], 0.0)
    t = m.transpose(ps[0][:, 0, 0:E], Wr[:, :], k["ident"][0:E, 0:E], t_in)
    w = m.copy(m.dve, WrT[:, 0:E], ps[0][:, 0, 0:E], t, z)
    m.memset(m.dve, off[0:64, :], 0.0)
    t_off = m.memset(m.dve, off[64:P, :], float(HALF))
    x1T_ready, free = [], [w, None]
    for q in range(T // 512):
        bank = ps[0][:, q % 2, :]
        for n in range(4):
            t = m.transpose(bank[:, n * P:(n + 1) * P], x1[:, 4 * q + n, :], k["ident"][:, :], free[q % 2],
                            signal=n == 3)
        free[q % 2] = m.copy(m.dve, x1T[:, q * 512:(q + 1) * 512], bank, t)
        x1T_ready.append(free[q % 2])
    for c in range(HALF // 512):
        out = ps[1 + c // 2][:, c % 2, :]
        m.matmul(out[0:64, :], WrT[:, :], x1T[:, c * 512:(c + 1) * 512], w, x1T_ready[-1])
        t = m.matmul(out[64:P, :], WrT[:, :], x1T[:, HALF + c * 512:HALF + (c + 1) * 512])
        last = m.copy(m.dve, L[:, c * 512:(c + 1) * 512], out, t)
    for r in range(C // 8):
        eight = slice(8 * r, 8 * r + 8)
        t = m.dve.do(lambda e, s=eight: e.max(vals[:, s], L[:, :]), last)
        t = m.dve.do(lambda e, s=eight: e.max_index(idx[:, s], vals[:, s], L[:, :]), t)
        last = m.dve.do(lambda e, s=eight: e.match_replace(L[:, :], vals[:, s], L[:, :], -3.0e38), t)
    t = m.copy(m.dve, idxf[:, :], idx[:, :], last)
    t = m.scalar_op(m.dve, idxf[:, :], idxf[:, :], off[:, 0:1], None, ALU.add, None, t, t_off)
    m.transpose(ps[0][:, 0, 0:P], vals[:, :], k["ident"][:, :], t)
    t = m.transpose(ps[0][:, 0, P:2 * P], idxf[:, :], k["ident"][:, :])
    m.copy(m.dve, vT[:, :], ps[0][:, 0, 0:P], t)
    t = m.copy(m.dve, iT[:, :], ps[0][:, 0, P:2 * P])
    m.matmul(ps[3][:, 0, 0:E], k["mirror"][:, :], vT[:, 64:64 + E], t)
    t = m.matmul(ps[3][:, 0, 64:64 + E], k["mirror"][:, :], iT[:, 64:64 + E])
    m.copy(m.dve, vB[:, :], ps[3][:, 0, 0:E], t)
    t = m.copy(m.dve, iB[:, :], ps[3][:, 0, 64:64 + E])
    m.tensor_op(m.dve, ge[:, :], vT[:, 0:E], vB[:, :], ALU.is_ge, t)
    m.tensor_op(m.dve, best[:, :], vT[:, 0:E], vB[:, :], ALU.max)
    t = m.tensor_op(m.dve, dif[:, :], iT[:, 0:E], iB[:, :], ALU.subtract)
    t = m.tensor_op(m.dve, dif[:, :], dif[:, :], ge[:, :], ALU.mult, t)
    t = m.tensor_op(m.dve, pick[:, :], dif[:, :], iB[:, :], ALU.add, t)
    m.routed = m.copy(m.dve, m.token[:, :], pick[:, :], t)
    t = m.transpose(ps[0][0:E, 1, 0:C], best[:, :], k["ident"][:, :], m.routed)
    a = m.copy(m.dve, rows[:, :], ps[0][0:E, 1, 0:C], t)
    t = m.dve.do(lambda e: e.tensor_reduce(mx[:, :], rows[:, :], AX_X, ALU.max), a)
    t = m.scalar_op(m.dve, rows[:, :], rows[:, :], mx[:, 0:1], None, ALU.subtract, None, t)
    t = m.activate(ex[:, :], rows[:, :], ACT.Exp, t, bias=k["eps"][0:E, 2:3], accum_out=sm[:, 0:1])
    t = m.dve.do(lambda e: e.reciprocal(rs[:, :], sm[:, :]), t)
    t = m.scalar_op(m.dve, ex[:, :], ex[:, :], rs[:, 0:1], None, ALU.mult, None, t)
    t = m.transpose(ps[3][:, 1, 0:E], ex[:, :], k["ident"][0:E, 0:E], t)
    m.share_ready = m.copy(m.dve, m.share[:, :], ps[3][:, 1, 0:E], t)


NACC = 4


def experts(m, d):
    E, NS, D, M = d["W1"].shape
    K = d["W2"].shape[3]
    k, sb = m.k, m.stage_sb
    NB = 4
    xg = sb("e_xg", [P, NB, D])
    xgT = sb("e_xgT", [P, NB, P])
    W1 = sb("e_W1", [P, NB, NS, M])
    W2 = sb("e_W2", [P, NB, NS, K])
    b2 = sb("e_b2", [1, NB, NS * K])
    b1r = sb("e_b1r", [P, 2, M])
    b1T = sb("e_b1T", [P, E * NS])
    hT = sb("e_hT", [P, NB, NS, P])
    y = sb("e_y", [P, NACC, NS * K])
    l_b1 = m.lane("e_l_b1")
    l_w = [m.lane(f"e_l_w{i}") for i in range(NB)]
    l_g = [m.lane(f"e_l_g{i}") for i in range(NB)]
    l_s = [m.lane(f"e_l_s{i}") for i in range(NACC)]
    half = E * NS // 2
    t_b1 = m.sp.dma(l_b1, b1r[0:half, :, :], d["b1"].rearrange("e s m -> (e s) m").rearrange("(a r) m -> r a m", a=2))
    for a in range(2):
        t = m.transpose(m.ps[0][:, 0, a * half:(a + 1) * half], b1r[0:half, a, :], k["ident"][0:half, 0:half], t_b1)
    t_b1T = m.copy(m.dve, b1T[:, :], m.ps[0][:, 0, 0:E * NS], t)
    t_w, t_g = {}, {}
    xg_used, w_used, y_sent = {}, {}, {}

    def load(e):
        i = e % NB
        m.sp.wait(w_used.get(e - NB))
        m.sp.dma(l_w[i], W1[:, i, :, :], d["W1"][e].rearrange("s d m -> d s m"))
        m.sp.dma(l_w[i], W2[:, i, :, :], d["W2"][e].rearrange("s m k -> m s k"))
        t_w[e] = m.sp.dma(l_w[i], b2[:, i, :], d["b2"][e].rearrange("(a s) k -> a (s k)", a=1))
        m.pool.wait(m.routed, *m.x1_stored, xg_used.get(e - NB))
        lane = l_g[i]
        lane.total += 16
        m.pool.queue.append(lambda g, e=e, i=i, lane=lane: g.indirect_dma_start(
            xg[:, i, :], None, m.x1_dram[:, :], bass.IndirectOffsetOnAxis(m.token[:, e:e + 1], 0)).then_inc(lane.sem, 16))
        t_g[e] = (lane.sem, lane.total)

    evac = {}
    ps_free = {}

    def transpose_in(e):
        i = e % NB
        bank = m.ps[0][:, e % 2, 0:P]
        t = m.transpose(bank, xg[:, i, :], k["ident"][:, :], t_g[e], ps_free.get(("x", e % 2)), t_b1T)
        xg_used[e] = t
        v = m.copy(m.dve, xgT[:, i, :], bank, t, w_used.get(e - NB))
        ps_free["x", e % 2] = v
        evac[e] = v

    def hidden(e):
        i = e % NB
        bank = m.ps[1][:, e % 2, :]
        for s in range(NS):
            t = m.matmul(bank[:, s * P:(s + 1) * P], W1[:, i, s, :], xgT[:, i, :], t_w[e], evac[e],
                         ps_free.get(("h", e % 2)), signal=s == NS - 1)
        for s in range(NS):
            a = m.activate(hT[:, i, s, :], bank[:, s * P:(s + 1) * P], ACT.Gelu, t, t_b1T, w_used.get(e - NB),
                           bias=b1T[:, e * NS + s:e * NS + s + 1])
        ps_free["h", e % 2] = a
        return a

    def output(e, a):
        i, j = e % NB, e % NACC
        bank = m.ps[2][:, e % 2, 0:NS * K]
        t = m.matmul(bank, k["ones"][0:1, :], b2[:, i, :], t_w[e], ps_free.get(("y", e % 2)), start=True, stop=False,
                     signal=False)
        for s in range(NS):
            t = m.matmul(bank[:, s * K:(s + 1) * K], hT[:, i, s, :], W2[:, i, s, :], a, start=False, stop=s == NS - 1,
                         signal=s == NS - 1)
        w_used[e] = t
        v = m.scalar_op(m.dve, y[:, j, :], bank, m.share[:, e:e + 1], None, ALU.mult, None, t, m.share_ready,
                        y_sent.get(e - NACC))
        ps_free["y", e % 2] = v
        lane = l_s[j]
        m.pool.wait(v, y_sent.get(e - NACC), *m.x1_stored, m.zeroed)
        lane.total += 16
        m.pool.queue.append(lambda g, e=e, j=j, lane=lane: g.indirect_dma_start(
            m.acc_dram[j][:, :], bass.IndirectOffsetOnAxis(m.token[:, e:e + 1], 0), y[:, j, :], None,
            compute_op=ALU.add).then_inc(lane.sem, 16))
        y_sent[e] = (lane.sem, lane.total)

    act_done = {}
    for e in range(NB - 1):
        load(e)
    for e in range(E + 1):
        if e < E:
            transpose_in(e)
            act_done[e] = hidden(e)
        if e > 0:
            output(e - 1, act_done[e - 1])
        if e + NB - 1 < E:
            load(e + NB - 1)
    m.scattered = [y_sent[e] for e in range(E - NACC, E)]


def join_experts(m, x2):
    NTT = x2.shape[1]
    NT = 4
    sb = m.stage_sb
    A = sb("j_A", [P, 2, NACC, NT, P])
    tmp = ln_buffers(sb, "j_ln", NT)
    lanes = [m.lane(f"j_l{i}") for i in range(2)]
    used = {}
    t_in = {}

    def load(b):
        m.sp.wait(*m.scattered, used.get(b - 2))
        for j in range(NACC):
            t_in[b] = m.sp.dma(lanes[b % 2], A[:, b % 2, j, :, :],
                               m.acc_dram[j][b * NT * P:(b + 1) * NT * P, :].rearrange("(n p) d -> p n d", p=P))

    NBATCH = NTT // NT
    load(0)
    load(1)
    for b in range(NBATCH):
        a = A[:, b % 2]
        m.tensor_op(m.dve, a[:, 0], a[:, 0], a[:, 1], ALU.add, t_in[b])
        t = m.tensor_op(m.pool, a[:, 2], a[:, 2], a[:, 3], ALU.add, t_in[b])
        m.dve.wait((m.dve.sem, m.dve.count))
        t = m.tensor_op(m.dve, a[:, 0], a[:, 0], a[:, 2], ALU.add, t)
        used[b] = m.x2_ready = layernorm_rows(m, a[:, 0], x2[:, b * NT:(b + 1) * NT, :], tmp, NT, t)
        if b + 2 < NBATCH:
            load(b + 2)


def relative_attention(m, d, x2, x3):
    B, T, D, H = 8, 512, 128, 16
    DH = D // H
    NT = T // P
    HB = H // 2
    SCALE = float(DH) ** -0.5
    LEFT = [(0, 0, 3), (1, 3, 2), (2, 5, 1)]
    RIGHT = [(0, 0), (1, 1), (2, 2), (0, 3), (1, 4), (0, 5)]
    ROWS = 6 * DH
    BF16 = mybir.dt.bfloat16
    k, sb = m.k, m.stage_sb
    Wq, Wk, Wp, Wv, Wo = (sb("c_" + n, [P, D]) for n in ("Wq", "Wk", "Wp", "Wv", "Wo"))
    rows = sb("c_rows", [1, 6, D])
    cols = sb("c_cols", [P, 6])
    bv, bo = sb("c_bv", [P, D]), sb("c_bo", [P, D])
    peT = sb("c_peT", [P, T])
    XN = sb("c_XN", [P, NT, D])
    XNT = sb("c_XNT", [P, T])
    PART = sb("c_PART", [P, 3, 3, T], BF16)
    RES = sb("c_RES", [P, 2, T])
    QU = sb("c_QU", [P, 2, HB, T], BF16)
    QV = sb("c_QV", [P, 2, HB, T], BF16)
    KR = sb("c_KR", [P, 2, HB // 2, T], BF16)
    PR = sb("c_PR", [P, H // 2, T], BF16)
    V = sb("c_V", [P, 2, NT, H, 32])
    fold = sb("c_fold", [P, DH + 1])
    NU, NK = 2, 3
    U = sb("c_U", [P, NU, NT, T + 1])
    SK = sb("c_SK", [P, NK, NT, T])
    TS = sb("c_TS", [P, 2, NT, T])
    MX = sb("c_MX", [P, 2, NT])
    EX = sb("c_EX", [P, 2, NT, T])
    OT = sb("c_OT", [P, T])
    RS = sb("c_RS", [P, NT, 4])
    HD = sb("c_HD", [P, NT, H, DH])
    HDT = sb("c_HDT", [P, T])
    Y = sb("c_Y", [P, NT, D])
    tmp = ln_buffers(sb, "c_ln", NT)
    tmp2 = ln_buffers(sb, "c_ln2", NT)
    u_ps = [m.ps[0][:, 0, :], m.ps[0][:, 1, :]]
    c_ps = [m.ps[1][:, 0, :], m.ps[1][:, 1, :]]
    t_ps = m.ps[2]
    o_ps, j_ps = m.ps[3][:, 0, :], m.ps[3][:, 1, :]
    G = 4
    n_view = j_ps[:, 0:G * NT * (DH + 1)].rearrange("p (g n c) -> p g n c", g=G, n=NT)

    l_in = m.lane("c_l_in")
    for tile, name in ((Wq, "Wq"), (Wk, "Wk"), (Wp, "Wp"), (Wv, "Wv"), (Wo, "Wo")):
        m.sp.dma(l_in, tile[:, :], d[name])
    for n, name in enumerate(("bq", "bk", None, None, "ln_g", "ln_b")):
        if name:
            m.sp.dma(l_in, rows[:, n, :], d[name].rearrange("(a e) -> a e", a=1))
    m.sp.dma(l_in, rows[:, 2, :], d["u_bias"].rearrange("(a h) e -> a (h e)", a=1))
    m.sp.dma(l_in, rows[:, 3, :], d["v_bias"].rearrange("(a h) e -> a (h e)", a=1))
    m.sp.dma(l_in, bv[:, :], d["bv"].rearrange("(a e) -> a e", a=1).broadcast_to([P, D]))
    m.sp.dma(l_in, bo[:, :], d["bo"].rearrange("(a e) -> a e", a=1).broadcast_to([P, D]))
    t_in = m.sp.dma(l_in, peT[:, :], d["peT"])

    m.memset(m.pool, U[:, :, :, 0:1], 0.0)
    m.memset(m.pool, QU[:, :, :, :], 0.0)
    m.memset(m.pool, QV[:, :, :, :], 0.0)
    m.memset(m.pool, KR[:, :, :, :], 0.0)
    m.memset(m.pool, PR[:, :, :], 0.0)
    m.memset(m.pool, V[:, :, :, :, DH + 1:32], 0.0)
    m.memset(m.pool, V[:, :, :, :, DH:DH + 1], 1.0)
    m.memset(m.pool, fold[:, :], 0.0)
    for q in range(4):
        z = m.pool.do(lambda e, q=q: e.affine_select(
            out=fold[:, :], in_=fold[:, :], compare_op=ALU.not_equal, fill=1.0, base=-32 * q,
            pattern=[[-1, DH + 1]], channel_multiplier=1))

    m.tensor_op(m.dve, rows[:, 2, :], rows[:, 0, :], rows[:, 2, :], ALU.add, t_in)
    t = m.tensor_op(m.dve, rows[:, 3, :], rows[:, 0, :], rows[:, 3, :], ALU.add)
    for n, src in enumerate((2, 3, 1, 4, 5)):
        c = m.matmul(j_ps[:, n:n + 1], rows[:, src, :], k["ones"][0:1, 0:1], t)
    cols_ready = m.copy(m.dve, cols[:, 0:5], j_ps[:, 0:5], c)
    st = {"j": cols_ready, "t": None, "u": [None, None], "c": [None, None], "o": None, "ot": None}
    part_sent = [None]
    stack_lane = m.lane("c_l_parts")
    stack_used = {}

    def split(n, bank, bias, t):
        hi = m.activate(PART[:, n, 0, :], bank, ACT.Identity, t, cols_ready, part_sent[0], bias=bias)
        m.dve.wait(hi, split_used[n % 2])
        left = m.dve.do(lambda e: e.scalar_tensor_tensor(RES[:, n % 2, :], bank, bias, PART[:, n, 0, :],
                                                        ALU.add, ALU.subtract), t)
        mid = m.activate(PART[:, n, 1, :], RES[:, n % 2, :], ACT.Copy, left)
        low = m.tensor_op(m.dve, PART[:, n, 2, :], RES[:, n % 2, :], PART[:, n, 1, :], ALU.subtract, mid)
        split_used[n % 2] = low
        return left, low

    split_used = [None, None]

    def stack_rows(n):
        return m.stack_dram[n].rearrange("(h j e) t -> j h e t", j=6, e=DH)

    def send_parts(n, left, *needs):
        for j, part in enumerate((0, 0, 0, 1, 1, 2) if left else (0, 1, 2, 0, 1, 0)):
            t = m.sp.dma(stack_lane, stack_rows(n)[j], PART[:, n, part, :], *needs)
        return t

    def stack_half(n, half, odd):
        v = m.stack_dram[n].rearrange("(q o r) t -> o r q t", o=2, r=ROWS)[odd]
        return v[:, half * (HB // 2):(half + 1) * (HB // 2), :]

    t = m.matmul(j_ps, Wp[:, :], peT[:, :], t_in, st["j"])
    m.memset(m.dve, cols[:, 5:6], 0.0)
    m.act.wait((m.dve.sem, m.dve.count))
    m.dve.wait((m.dve.sem, m.dve.count))
    left, low = split(2, j_ps, cols[:, 5:6], t)
    st["j"] = left
    part_sent[0] = t = send_parts(2, False, low)
    for odd in range(2):
        v = m.stack_dram[2].rearrange("(q o r) t -> o r q t", o=2, r=ROWS)[odd]
        t = m.sp.dma(stack_lane, PR[64 * odd:64 * odd + ROWS, :, :], v, t, z)
        pr_loaded = t
    m.sp.wait(t)
    sent_read = [t]

    l_store = [m.lane(f"c_l_store{i}") for i in range(NU)]
    l_fetch = [m.lane(f"c_l_fetch{i}") for i in range(NK)]
    l_stack = [m.lane(f"c_l_stack{i}") for i in range(2)]
    stored, fetched, sk_used = {}, {}, {}
    ts_ready, ts_used, ex_ready, pv_done, hd_used = {}, {}, {}, {}, [None]
    stacks, sent, v_ready, users = {}, {}, {}, {}

    def prepare(b):
        x = x2[:, b * NT:(b + 1) * NT, :]
        r = layernorm_rows(m, x, XN, tmp, NT, m.x2_ready, st.get("xn"))
        for n in range(NT):
            t = m.transpose(j_ps[:, n * P:(n + 1) * P], XN[:, n, :], k["ident"][:, :], r, st["j"], signal=n == NT - 1)
        st["xn"] = t
        xt = m.scalar_op(m.dve, XNT[:, :], j_ps, cols[:, 3:4], cols[:, 4:5], ALU.mult, ALU.add, t, cols_ready,
                         st.get("xnt"))
        st["j"] = xt
        t = m.matmul(j_ps, Wq[:, :], XNT[:, :], xt)
        _, low = split(0, j_ps, cols[:, 0:1], t)
        left, low = split(1, j_ps, cols[:, 1:2], t)
        send_parts(0, True, low, sent_read[0])
        send_parts(1, True, low)
        t = m.matmul(j_ps, Wk[:, :], XNT[:, :], left)
        left, low = split(2, j_ps, cols[:, 2:3], t)
        sent[b] = part_sent[0] = send_parts(2, False, low)
        for n in range(NT):
            t = m.matmul(j_ps[:, n * P:(n + 1) * P], XNT[:, n * P:(n + 1) * P], Wv[:, :], left)
        st["xnt"] = t
        for n in range(NT):
            v = m.tensor_op(m.dve, V[:, b % 2, n, :, 0:DH], j_ps[:, n * P:(n + 1) * P].rearrange("p (h e) -> p h e", h=H),
                            bv[:, :].rearrange("p (h e) -> p h e", h=H), ALU.add, t, users.get((b - 2, "pv")), z)
        st["j"] = v_ready[b] = v

    def load_stacks(c):
        b, half = divmod(c, 2)
        i = c % 2
        used = [stack_used.get((c - 2, kind)) for kind in ("pos", "content")]
        for odd in range(2):
            rs = slice(64 * odd, 64 * odd + ROWS)
            for tile, n, step in ((QV, 1, 2), (QU, 0, 2), (KR, 2, 1)):
                dst = tile[rs, i, odd:HB:2, :] if step == 2 else tile[rs, i, :, :]
                t = m.sp.dma(l_stack[i], dst, stack_half(n, half, odd), sent[b], z, *used)
        stacks[c] = t
        if half:
            m.sp.wait(stacks[c - 1], t)
            sent_read[0] = t

    def positions(w, n):
        b, h = divmod(w, H)
        c, g = w // HB, h % HB
        i, j2, j = w % NU, w % NK, n % 2
        t = m.matmul(u_ps[j], QV[:, c % 2, g, n * P:(n + 1) * P], PR[:, h // 2, :], stacks[c], pr_loaded, st["u"][j])
        a = st["u"][j] = m.activate(U[:, i, n, 1:T + 1], u_ps[j], ACT.Copy, t, z, stored.get(w - NU))
        if n == NT - 1:
            stack_used[c, "pos"] = t
            stored[w] = m.act.dma(l_store[i], m.shift_dram[j2].rearrange("(n p) c -> p n c", p=P), U[:, i, :, :], a,
                                 fetched.get(w - NK))

    def fetch(w):
        j2 = w % NK
        flat = m.shift_dram[j2].rearrange("a c -> (a c)")[T:T + T * T]
        fetched[w] = m.sp.dma(l_fetch[j2], SK[:, j2, :, :], flat.rearrange("(n p c) -> p n c", p=P, c=T), stored[w],
                              sk_used.get(w - NK))

    def scores(w, n):
        b, h = divmod(w, H)
        c, g = w // HB, h % HB
        i, s, j = w % NK, w % 2, n % 2
        t = m.matmul(c_ps[j], QU[:, c % 2, g, n * P:(n + 1) * P], KR[:, c % 2, g // 2, :], stacks[c], st["c"][j])
        m.dve.wait(t, fetched[w], ts_used.get(w - 2))
        v = st["c"][j] = m.dve.do(lambda e: e.tensor_tensor_reduce(
            TS[:, s, n, :], c_ps[j], SK[:, i, n, :], 1.0, -3.0e38, ALU.add, ALU.max, MX[:, s, n:n + 1]))
        stack_used[c, "content"] = t
        sk_used[w] = v

    def less_max(w):
        s = w % 2
        for n in range(NT):
            v = m.scalar_op(m.dve, TS[:, s, n, :], TS[:, s, n, :], MX[:, s, n:n + 1], None, ALU.subtract, None,
                            sk_used[w])
        ts_ready[w] = v

    def turn_exp(w, half):
        s = w % 2
        for c in range(2):
            jb = 2 * half + c
            for n in range(NT):
                t = m.transpose(t_ps[:, c, n * P:(n + 1) * P], TS[:, s, n, jb * P:(jb + 1) * P], k["ident"][:, :],
                                ts_ready[w], st["t"], signal=n == NT - 1)
        a = m.activate(EX[:, s, 2 * half:2 * half + 2, :], t_ps[:, :, :], ACT.Exp, t, pv_done.get(w - 2),
                       scale=SCALE, bias=k["eps"][:, 2:3])
        st["t"] = a
        ts_used[w] = t
        ex_ready[w] = a

    def apply(w):
        b, h = divmod(w, H)
        for jb in range(NT):
            t = m.matmul(o_ps[32 * jb:32 * jb + 32, :], V[:, b % 2, jb, h, :], EX[:, w % 2, jb, :], ex_ready[w],
                         v_ready[b], st["o"])
        pv_done[w] = users[b, "pv"] = t
        ot_ready[w] = st["o"] = m.copy(m.dve, OT[:, :], o_ps, t, st["ot"])

    def fold_apply(w):
        b, h = divmod(w, H)
        g, r = divmod(h, G)
        for n in range(NT):
            t = m.matmul(n_view[:, r, n, :], OT[:, n * P:(n + 1) * P], fold[:, :], ot_ready[w], st["j"])
        st["ot"] = t
        if r == G - 1:
            v = m.dve.do(lambda e: e.reciprocal(RS[:, :, :], n_view[:, :, :, DH].rearrange("p g n -> p n g")), t)
            for n in range(NT):
                t = m.tensor_op(m.dve, HD[:, n, g * G:(g + 1) * G, :], n_view[:, :, n, 0:DH],
                                RS[:, n, :].unsqueeze(2).broadcast_to([P, G, DH]), ALU.mult, v, hd_used[0])
            st["j"] = t
            if h == H - 1:
                finish(b, t)

    ot_ready = {}

    def finish(b, hd_ready):
        x = x2[:, b * NT:(b + 1) * NT, :]
        for n in range(NT):
            xb = m.tensor_op(m.pool, Y[:, n, :], x[:, n, :], bo[:, :], ALU.add, m.x2_ready, t_in, st.get("y"))
            t = m.transpose(j_ps[:, n * P:(n + 1) * P], HD[:, n, :, :].rearrange("p h e -> p (h e)"),
                            k["ident"][:, :], hd_ready, st["j"], signal=n == NT - 1)
        hd_used[0] = t
        st["j"] = v = m.copy(m.dve, HDT[:, :], j_ps, t, st.get("hdt"))
        for n in range(NT):
            t = m.matmul(j_ps[:, n * P:(n + 1) * P], HDT[:, n * P:(n + 1) * P], Wo[:, :], v)
        st["hdt"] = t
        st["j"] = v = m.tensor_op(m.dve, Y[:, :, :], j_ps.rearrange("p (n c) -> p n c", n=NT), Y[:, :, :],
                                  ALU.add, t, xb)
        m.x3_ready = st["y"] = layernorm_rows(m, Y, x3[:, b * NT:(b + 1) * NT, :], tmp2, NT, v)

    W = B * H
    LEAD = 3
    m.load_table("natural_log_exp_and_others")
    prepare(0)
    load_stacks(0)
    for step in range(W + LEAD + 3):
        new, now, turned, applied = step, step - LEAD, step - LEAD - 1, step - LEAD - 2
        if 0 < step <= W:
            fetch(step - 1)
        for half in range(2):
            for n in (2 * half, 2 * half + 1):
                if new < W:
                    positions(new, n)
                if 0 <= now < W:
                    scores(now, n)
            if 0 <= turned < W:
                turn_exp(turned, half)
            if half == 0 and 0 <= applied < W:
                apply(applied)
        if 0 <= now < W:
            less_max(now)
        w = applied
        if 0 <= w < W:
            fold_apply(w)
            if w % HB == 0 and (w // HB) % 2 == 0:
                load_stacks(w // HB + 1)
            if w % H == H - 9 and w // H + 1 < B:
                prepare(w // H + 1)
            if w % H == H - 8 and w // H + 1 < B:
                load_stacks(2 * (w // H) + 2)


def gated_ffn(m, d, x3, out):
    NTT = x3.shape[1]
    D, E = d["gate_w"].shape
    NT = 4
    k, sb = m.k, m.stage_sb
    raw = sb("f_raw", [P, 2, D])
    WT = sb("f_WT", [P, 2 * D + E])
    bb = sb("f_bb", [P, 2 * D])
    XT = sb("f_XT", [P, NTT, P])
    PRE = sb("f_PRE", [P, NTT, 2 * D])
    LG = sb("f_LG", [P, NTT, E])
    red = sb("f_red", [P, NTT])
    inv = sb("f_inv", [P, NTT])
    cmp = sb("f_cmp", [P, NTT, E])
    rank, m0, m1 = sb("f_rank", [P, NTT]), sb("f_m0", [P, NTT]), sb("f_m1", [P, NTT])
    coef = sb("f_coef", [P, 2, NTT])
    Y = sb("f_Y", [P, NTT, D])
    O = sb("f_O", [P, NTT, D])
    tmp = ln_buffers(sb, "f_ln", NTT)
    lane, l_out = m.lane("f_l"), m.lane("f_l_out")
    m.sp.dma(lane, raw[:, 0, :], d["w0"])
    m.sp.dma(lane, raw[:, 1, :], d["w1"])
    m.sp.dma(lane, WT[:, 2 * D:2 * D + E], d["gate_w"])
    m.sp.dma(lane, bb[:, 0:D], d["b0"].rearrange("(a e) -> a e", a=1).broadcast_to([P, D]))
    t_in = m.sp.dma(lane, bb[:, D:2 * D], d["b1"].rearrange("(a e) -> a e", a=1).broadcast_to([P, D]))
    for n in range(2):
        t = m.transpose(m.ps[0][:, 0, n * P:(n + 1) * P], raw[:, n, :], k["ident"][:, :], t_in)
    w = m.copy(m.dve, WT[:, 0:2 * D], m.ps[0][:, 0, 0:2 * D], t)
    free = {"x0": w, "x1": None, "m0": None, "m1": None}
    for q in range(NTT // NT):
        key = f"x{q % 2}"
        bank = m.ps[0][:, q % 2, :]
        for n in range(NT):
            t = m.transpose(bank[:, n * P:(n + 1) * P], x3[:, q * NT + n, :], k["ident"][:, :], free[key],
                            signal=n == NT - 1)
        free[key] = xt = m.copy(m.dve, XT[:, q * NT:(q + 1) * NT, :], bank.rearrange("p (n c) -> p n c", n=NT), t)
        for n in range(NT):
            i = q * NT + n
            key2 = f"m{n % 2}"
            ps = m.ps[1][:, n % 2, 0:2 * D + E]
            t = m.matmul(ps, XT[:, i, :], WT[:, :], xt, w, free[key2])
            m.copy(m.dve, LG[:, i, :], ps[:, 2 * D:2 * D + E], t)
            free[key2] = pre = m.tensor_op(m.dve, PRE[:, i, :], ps[:, 0:2 * D], bb[:, :], ALU.add)

    def over_experts(col):
        return col.unsqueeze(2).broadcast_to([P, NTT, E])

    t = m.dve.do(lambda e: e.tensor_reduce(red[:, :], LG[:, :, :], AX_X, ALU.max), pre)
    t = m.tensor_op(m.dve, LG[:, :, :], LG[:, :, :], over_experts(red[:, :]), ALU.subtract, t)
    t = m.activate(LG[:, :, :], LG[:, :, :], ACT.Exp, t, bias=k["eps"][:, 2:3])
    t = m.dve.do(lambda e: e.tensor_reduce(red[:, :], LG[:, :, :], AX_X, ALU.add), t)
    t = m.dve.do(lambda e: e.reciprocal(inv[:, :], red[:, :]), t)
    t = m.tensor_op(m.dve, LG[:, :, :], LG[:, :, :], over_experts(inv[:, :]), ALU.mult, t)
    t = m.dve.do(lambda e: e.tensor_reduce(red[:, :], LG[:, :, 1:E], AX_X, ALU.max), t)
    t = m.tensor_op(m.dve, m0[:, :], LG[:, :, 0], red[:, :], ALU.is_ge, t)
    m.tensor_op(m.dve, coef[:, 0, :], LG[:, :, 0], m0[:, :], ALU.mult, t)
    m.tensor_op(m.dve, cmp[:, :, 2:E], LG[:, :, 2:E], LG[:, :, 1:2].broadcast_to([P, NTT, E - 2]), ALU.is_gt)
    t = m.tensor_op(m.dve, cmp[:, :, 1], LG[:, :, 0], LG[:, :, 1], ALU.is_ge)
    t = m.dve.do(lambda e: e.tensor_reduce(rank[:, :], cmp[:, :, 1:E], AX_X, ALU.add), t)
    t = m.scalar_op(m.dve, m1[:, :], rank[:, :], 1.0, None, ALU.is_equal, None, t)
    c = m.tensor_op(m.dve, coef[:, 1, :], LG[:, :, 1], m1[:, :], ALU.mult, t)
    for q in range(NTT // NT):
        tiles = slice(q * NT, (q + 1) * NT)
        a = m.activate(PRE[:, tiles, :], PRE[:, tiles, :], ACT.Silu, pre)
        for i in range(q * NT, (q + 1) * NT):
            t = m.scalar_op(m.dve, Y[:, i, :], PRE[:, i, 0:D], coef[:, 0, i:i + 1], None, ALU.mult, None, a, c)
            m.dve.wait(t)
            t = m.dve.do(lambda e, i=i: e.scalar_tensor_tensor(Y[:, i, :], PRE[:, i, D:2 * D], coef[:, 1, i:i + 1],
                                                              Y[:, i, :], ALU.mult, ALU.add))
        t = m.tensor_op(m.dve, Y[:, tiles, :], Y[:, tiles, :], x3[:, tiles, :], ALU.add, t)
    r = layernorm_rows(m, Y, O, tmp, NTT, t)
    t = m.sp.dma(l_out, out.rearrange("b (n p) d -> p (b n) d", p=P), O[:, :, :], r)
    m.sp.wait(t)


def two_layers_kernel(nc, ins, out):
    B, T, D = ins["L0_attn_X"].shape
    rows = B * T
    NTT = rows // P

    def part(prefix):
        return {n[len(prefix):]: ap for n, ap in ins.items() if n.startswith(prefix)}

    with ExitStack() as ctx:
        m = Machine(nc, ctx)
        m.ps = [ctx.enter_context(nc.psum_tensor(f"ps{i}", [P, 2, 512], F32)) for i in range(4)]
        m.x1_dram = nc.dram_tensor("x1_dram", (rows, D), F32, kind="Internal").ap()
        m.acc_dram = [nc.dram_tensor(f"acc_dram{j}", (rows, D), F32, kind="Internal").ap() for j in range(NACC)]
        m.shift_dram = [nc.dram_tensor(f"shift_dram{j}", (T, T + 1), F32, kind="Internal").ap() for j in range(3)]
        m.stack_dram = [nc.dram_tensor(f"stack_dram{j}", (16 * 48, T), mybir.dt.bfloat16, kind="Internal").ap()
                        for j in range(3)]
        make_constants(m)
        xA = m.sb("x_a", [P, NTT, D])
        m.token = m.sb("token", [P, 48], U32)
        m.share = m.sb("share", [P, 48])

        with ExitStack() as x1_ctx:
            zeros = x1_ctx.enter_context(nc.sbuf_tensor("zeros", [P, 4 * D], F32))
            z = m.memset(m.pool, zeros[:, :], 0.0)
            l_zero = m.lane("l_zero")
            for j in range(1, NACC):
                for q in range(NTT // 4):
                    m.zeroed = m.sp.dma(l_zero, m.acc_dram[j][q * 4 * P:(q + 1) * 4 * P, :]
                                        .rearrange("(p n) d -> p (n d)", p=P), zeros[:, :], z)
            with ExitStack() as m.stage_ctx:
                m.stage("dist")
                distance_attention(m, part("L0_attn_"), xA)
                m.close_stage()
            with ExitStack() as m.stage_ctx:
                m.stage("route")
                route(m, part("L0_ffn_"), xA)
                m.close_stage()
            with ExitStack() as m.stage_ctx:
                m.stage("experts")
                experts(m, part("L0_ffn_"))
                m.close_stage()
        xB = m.sb("x_b", [P, NTT, D])
        with ExitStack() as m.stage_ctx:
            m.stage("join")
            join_experts(m, xA)
            m.close_stage()
        with ExitStack() as m.stage_ctx:
            m.stage("rel")
            relative_attention(m, dict(part("L1_attn_"), peT=ins["peT"]), xA, xB)
            m.close_stage()
        with ExitStack() as m.stage_ctx:
            m.stage("ffn")
            gated_ffn(m, part("L1_ffn_"), xB, out)

        with nc.Block() as block:
            block.sync(lambda e: m.sp.play(e))
            block.gpsimd(lambda e: m.pool.play(e))
            block.scalar(lambda e: m.act.play(e))
            block.vector(lambda e: m.dve.play(e))
            block.tensor(lambda e: m.pe.play(e))


_INS = ["L0_attn_X", "L0_attn_W_in", "L0_attn_b_in", "L0_attn_W_out", "L0_attn_b_out", "L0_ffn_Wr", "L0_ffn_W1",
        "L0_ffn_b1", "L0_ffn_W2", "L0_ffn_b2", "L1_attn_ln_g", "L1_attn_ln_b", "L1_attn_Wq", "L1_attn_bq",
        "L1_attn_Wk", "L1_attn_bk", "L1_attn_Wv", "L1_attn_bv", "L1_attn_Wp", "L1_attn_Wo", "L1_attn_bo",
        "L1_attn_u_bias", "L1_attn_v_bias", "L1_ffn_gate_w", "L1_ffn_w0", "L1_ffn_b0", "L1_ffn_w1", "L1_ffn_b1"]


def position_table(length, width):
    pos = np.arange(length, dtype=np.float32)[:, None]
    div = np.exp(np.arange(0, width, 2, dtype=np.float32) * np.float32(-np.log(10000.0) / width)).astype(np.float32)
    ang = (pos * div).astype(np.float32)
    pe = np.stack([np.sin(ang), np.cos(ang)], axis=-1).reshape(length, width).astype(np.float32)
    return np.ascontiguousarray(pe.T)


def kernel(**inputs):
    import concourse.bacc as _bacc
    from concourse.bass_utils import run_bass_kernel_spmd as _run

    nc = _bacc.Bacc("TRN2", target_bir_lowering=False, num_devices=1)
    arrays, args = {}, {}
    for name in _INS:
        a = np.ascontiguousarray(inputs[name])
        arrays[f"in_{name}"] = a
        args[name] = nc.dram_tensor(f"in_{name}", a.shape, mybir.dt.from_np(a.dtype), kind="ExternalInput").ap()
    shape = tuple(inputs["L0_attn_X"].shape)
    peT = position_table(shape[1], shape[2])
    arrays["in_peT"] = peT
    args["peT"] = nc.dram_tensor("in_peT", peT.shape, F32, kind="ExternalInput").ap()
    out = nc.dram_tensor("out", shape, F32, kind="ExternalOutput").ap()
    two_layers_kernel(nc, args, out)
    r = _run(nc, [arrays], core_ids=[0])
    return r.results[0]["out"]
```

```python
from collections import deque
from contextlib import ExitStack

import numpy as np
import concourse.bass as bass
from concourse import mybir

ALU = mybir.AluOpType
ACT = mybir.ActivationFunctionType
F32 = mybir.dt.float32
U32 = mybir.dt.uint32
AX_X = mybir.AxisListType.X

P = 128
LN_EPS = 1e-5
POW_EPS = 1e-4


class Line:

    def __init__(self, name, new_sem, in_order=False):
        self.name, self.new_sem, self.in_order, self.last = name, new_sem, in_order, None
        self.queue, self.waited = [], {}
        self.stage("start")

    def stage(self, stage):
        self.sem, self.count = self.new_sem(f"{self.name}_{stage}"), 0

    def wait(self, *tickets):
        for t in tickets:
            if t is None:
                continue
            sem, value = t
            if self.waited.get(sem.name, 0) < value:
                self.waited[sem.name] = value
                self.queue.append(lambda e, s=sem, v=value: e.wait_ge(s, v))

    def do(self, emit, *needs, signal=True):
        self.wait(*needs, self.last if self.in_order else None)
        if not signal:
            self.queue.append(emit)
            return None
        self.count += 1
        sem = self.sem
        self.queue.append(lambda e: emit(e).then_inc(sem, 1))
        self.last = (sem, self.count)
        return self.last

    def dma(self, lane, out, in_, *needs):
        self.wait(*needs)
        lane.total += 16
        self.queue.append(lambda e: e.dma_start(out, in_).then_inc(lane.sem, 16))
        return (lane.sem, lane.total)

    def play(self, engine):
        for step in self.queue:
            step(engine)


class Lane:

    def __init__(self, sem):
        self.sem, self.total = sem, 0


class Machine:

    def __init__(self, nc, ctx):
        self.nc, self.ctx = nc, ctx
        self.pe = Line("pe", self.semaphore)
        self.act = Line("act", self.semaphore)
        self.dve = Line("dve", self.semaphore)
        self.pool = Line("pool", self.semaphore, in_order=True)
        self.sp = Line("sp", self.semaphore)
        self.stage_ctx = None

    def semaphore(self, name):
        return self.ctx.enter_context(self.nc.semaphore(name))

    def lane(self, name):
        return Lane(self.semaphore(name))

    def sb(self, name, shape, dt=F32):
        return self.ctx.enter_context(self.nc.sbuf_tensor(name, shape, dt))

    def stage_sb(self, name, shape, dt=F32):
        return self.stage_ctx.enter_context(self.nc.sbuf_tensor(name, shape, dt))

    def stage(self, name):
        for line in (self.pe, self.act, self.dve, self.pool, self.sp):
            line.stage(name)

    def close_stage(self):
        lines = (self.pe, self.act, self.dve, self.pool)
        last = [(line.sem, line.count) for line in lines if line.count]
        for line in lines + (self.sp,):
            line.wait(*[t for t in last if t[0] is not line.sem])
            line.wait(*[t for t in last if t[0] is line.sem])

    def matmul(self, out, lhsT, rhs, *needs, start=True, stop=True, signal=True):
        return self.pe.do(lambda e: e.matmul(out, lhsT, rhs, start=start, stop=stop), *needs, signal=signal)

    def transpose(self, out, in_, ident, *needs, signal=True):
        return self.pe.do(lambda e: e.transpose(out, in_, ident), *needs, signal=signal)

    def activate(self, out, in_, func, *needs, **kw):
        return self.act.do(lambda e: e.activation(out, in_, func, **kw), *needs)

    def load_table(self, name):
        self.act.do(lambda e: e.preload_act_table_set(name), signal=False)

    def scalar_op(self, line, out, in_, s1, s2, op0, op1, *needs):
        if op1 is None:
            return line.do(lambda e: e.tensor_scalar(out, in_, s1, None, op0), *needs)
        return line.do(lambda e: e.tensor_scalar(out, in_, s1, s2, op0, op1), *needs)

    def tensor_op(self, line, out, a, b, op, *needs):
        return line.do(lambda e: e.tensor_tensor(out, a, b, op), *needs)

    def copy(self, line, out, in_, *needs):
        return line.do(lambda e: e.tensor_copy(out, in_), *needs)

    def memset(self, line, out, value, *needs):
        return line.do(lambda e: e.memset(out, value), *needs)


def make_constants(m):
    k = m.k = {}
    k["ident"], k["ones"] = m.sb("ident", [P, P]), m.sb("ones", [P, P])
    k["eps"] = m.sb("eps_cols", [P, 4])
    a = m.memset(m.pool, k["ident"][:, :], 0.0)
    m.pool.wait(a)
    m.pool.do(lambda e: e.affine_select(out=k["ident"][:, :], in_=k["ident"][:, :], compare_op=ALU.not_equal,
                                        fill=1.0, base=0, pattern=[[-1, P]], channel_multiplier=1))
    m.memset(m.pool, k["ones"][:, :], 1.0)
    m.memset(m.pool, k["eps"][:, 0:1], POW_EPS)
    m.memset(m.pool, k["eps"][:, 1:2], LN_EPS)
    k["ready"] = m.memset(m.pool, k["eps"][:, 2:3], 0.0)


def row_moments(m, x, tmp, n, *needs):
    stats, mv = tmp[0:2]
    for i in range(n):
        t = m.dve.do(lambda e, i=i: e.bn_stats(stats[:, i, :], x[:, i, :]), *needs, *tmp[4])
    m.dve.wait(t)
    for i in range(n):
        t = m.dve.do(lambda e, i=i: e.bn_aggr(mv[:, i, :], stats[:, i, :]))
    return t


def inverse_deviation(m, tmp, n, t):
    _, mv, lg, rstd = tmp[0:4]
    t = m.activate(lg[:, 0:n], mv[:, 0:n, 1], ACT.Ln, t, m.k["ready"], bias=m.k["eps"][:, 1:2])
    return m.activate(rstd[:, 0:n], lg[:, 0:n], ACT.Exp, t, scale=-0.5, bias=m.k["eps"][:, 2:3])


def normalise_rows(m, x, out, tmp, n, t, *needs):
    mv, rstd = tmp[1], tmp[3]
    for i in range(n):
        r = m.scalar_op(m.dve, out[:, i, :], x[:, i, :], mv[:, i, 0:1], rstd[:, i:i + 1],
                        ALU.subtract, ALU.mult, t, *needs)
    tmp[4][:] = [r]
    return r


def ln_buffers(make, name, n):
    return (make(name + "_stats", [P, n, 6]), make(name + "_mv", [P, n, 2]),
            make(name + "_lg", [P, n]), make(name + "_rstd", [P, n]), [])


def distance_attention(m, d, x1):
    B, T, D = d["X"].shape
    H, E = 16, 64
    G = 4
    NG = H // G
    NT = T // P
    sb = m.stage_sb
    k = m.k
    W = sb("a_W_in", [P, 4, H, E])
    Wo = sb("a_W_out", [P, H // 2, D])
    brow = sb("a_b_rows", [4 * H, E])
    bcol = sb("a_b_cols", [P, H // 2, 4])
    bk2 = sb("a_bk_m2", [P, H // 2])
    bv = sb("a_bv", [P, H, E])
    bo = sb("a_bo", [P, D])
    pick = sb("a_pick", [P, 2, 32])
    X = sb("a_X", [P, 2, NT, D])
    XT = sb("a_XT", [P, T])
    QA = sb("a_QA", [E + 2, 2, G, T])
    KA = sb("a_KA", [E + 2, 2, G, T])
    GT = sb("a_GT", [P, 3, 2, T])
    V = sb("a_V", [P, 2, NT, G, E])
    SQ = sb("a_SQ", [P, 2, 2, T])
    sums_out = sb("a_sums_out", [P, T])
    S = sb("a_S", [P, 2, G, NT, T])
    W2 = sb("a_W2", [P, 2, T])
    WS = sb("a_WS", [P, G, T])
    RR = sb("a_RR", [P, 2, T])
    HT = sb("a_HT", [P, H // 2, T])
    tmp = ln_buffers(sb, "a_ln", NT)
    score_ps, pv_ps, prj_ps = m.ps[0:2], m.ps[2], m.ps[3]

    l_w, l_b, l_rest, l_x = [m.lane(f"a_l_w{c}") for c in range(4)], m.lane("a_l_b"), m.lane("a_l_rest"), [m.lane(f"a_l_x{i}") for i in range(2)]
    m.sp.dma(l_x[0], X[:, 0, :, :], d["X"][0].rearrange("(n p) d -> p n d", p=P))
    t_x = [(l_x[0].sem, l_x[0].total), None]
    m.sp.dma(l_b, brow[:, :], d["b_in"].rearrange("(r e) -> r e", e=E))
    t_b = (l_b.sem, l_b.total)
    t_w = {}
    for c in (0, 1, 3, 2):
        t_w[c] = m.sp.dma(l_w[c], W[:, c, :, :], d["W_in"].rearrange("p (h c e) -> p h c e", h=H, c=4)[:, :, c, :])
    m.sp.dma(l_rest, bv[:, :, :], d["b_in"].rearrange("(a h c e) -> a h c e", a=1, h=H, c=4)[:, :, 2, :]
             .broadcast_to([P, H, E]))
    m.sp.dma(l_rest, bo[:, :], d["b_out"].rearrange("(a e) -> a e", a=1).broadcast_to([P, D]))
    t_rest = m.sp.dma(l_rest, Wo[:, :, :], d["W_out"].rearrange("(q p) n -> p q n", p=P))

    t = m.memset(m.pool, pick[:, :, :], 0.0)
    m.pool.wait(t)
    for odd in range(2):
        half = slice(E * odd, E * odd + E)
        m.memset(m.pool, pick[half, 0, odd:odd + 1], 1.0)
        m.memset(m.pool, pick[half, 1, odd:odd + 1], 0.25)
    m.memset(m.pool, QA[E:E + 2, :, :, :], 1.0)
    m.memset(m.pool, KA[E:E + 2, :, :, :], 1.0)
    t_const = (m.pool.sem, m.pool.count)

    t = m.transpose(prj_ps[0:E, 0, 0:4 * H], brow[:, :], k["ident"][0:4 * H, 0:4 * H], t_b, k["ready"])
    src = prj_ps[0:E, 0, 0:4 * H].rearrange("p (q o c) -> p o q c", o=2, c=4)
    m.copy(m.dve, bcol[0:E, :, :], src[:, 0], t)
    t = m.copy(m.dve, bcol[E:P, :, :], src[:, 1])
    t_bc = m.scalar_op(m.dve, bk2[:, :], bcol[:, :, 1], -2.0, None, ALU.mult, None, t)

    prj_free = [t_bc, None]
    turn = {"prj": 1, "score": 0}
    score_free = [None, None]
    pv_free = [None, None]
    xT_ready, xT_used = {}, {}
    row_lane, rows_sent, rows_summed = [m.lane("a_l_q2"), m.lane("a_l_k2")], [None, None], [None]
    squared, projected, scored, values_ready = [None, None], {}, {}, {}
    S_used = [None, None]
    unit_ready, d2_done, w_done, pv_done = {}, {}, {}, {}
    gt_used = {}
    ht_used = [None]
    x_used = {}
    out_lane = [m.lane("a_l_x1d"), m.lane("a_l_acc")]

    def prj_bank():
        i = turn["prj"]
        turn["prj"] = 1 - i
        return i, prj_ps[:, i, :], prj_free[i]

    def load_x(b):
        if b < B and b > 0:
            t_x[b % 2] = m.sp.dma(l_x[b % 2], X[:, b % 2, :, :], d["X"][b].rearrange("(n p) d -> p n d", p=P),
                                  x_used.get(b - 2))

    def transpose_x(b):
        i, bank, free = prj_bank()
        for n in range(NT):
            t = m.transpose(bank[:, n * P:(n + 1) * P], X[:, b % 2, n, :], k["ident"][:, :], t_x[b % 2], free,
                            k["ready"], signal=n == NT - 1)
        xT_ready[b] = m.copy(m.dve, XT[:, :], bank, t, xT_used.get(b - 1))
        prj_free[i] = xT_ready[b]

    def project_pair(u, pr, parts=(0, 1, 3)):
        b, g = divmod(u, NG)
        s = u % 2
        q = 2 * g + pr
        for part in parts:
            i, bank, free = prj_bank()
            t = m.matmul(bank, W[:, part, 2 * q:2 * q + 2, :], XT[:, :], t_w[part], xT_ready[b], free)
            if part == 3:
                gate_ready[u, pr] = m.scalar_op(m.dve, GT[:, u % 3, pr, :], bank, bcol[:, q, 3:4], None, ALU.add, None,
                                                t, t_bc, gt_used.get(u - 3))
                prj_free[i] = gate_ready[u, pr]
                continue
            dst = (QA, KA)[part]
            for odd in range(2):
                rows = slice(E * odd, E * odd + E)
                if part == 0:
                    v = m.scalar_op(m.dve, QA[0:E, s, 2 * pr + odd, :], bank[rows, :], bcol[rows, q, 0:1], None,
                                    ALU.add, None, t, t_bc, scored.get(u - 2))
                else:
                    v = m.scalar_op(m.dve, KA[0:E, s, 2 * pr + odd, :], bank[rows, :], -2.0, bk2[rows, q:q + 1],
                                    ALU.mult, ALU.add, t, t_bc, scored.get(u - 2))
            projected[u] = prj_free[i] = v
            for odd in range(2):
                src = dst[0:E, s, 2 * pr + odd, :]
                squared[part] = m.tensor_op((m.pool, m.dve)[part], SQ[E * odd:E * odd + E, part, pr, :], src, src,
                                            ALU.mult, v, rows_summed[0])

    def square_rows(u):
        s = u % 2
        i, bank, free = prj_bank()
        for part in range(2):
            for pr in range(2):
                at = 32 * (2 * part + pr)
                t = m.matmul(bank[at:at + 32, :], pick[:, part, :], SQ[:, part, pr, :], squared[part], t_const, free)
        rows_summed[0] = t
        t = prj_free[i] = m.copy(m.dve, sums_out[:, :], bank, t, *rows_sent)
        for part, dst in ((0, QA), (1, KA)):
            row = E + part
            for pr in range(2):
                at = 32 * (2 * part + pr)
                rows_sent[part] = m.sp.dma(row_lane[part],
                                           dst[row:row + 1, s, 2 * pr:2 * pr + 2, :].rearrange("a g t -> a (g t)"),
                                           sums_out[at:at + 2, :], t, t_const, scored.get(u - 2))
        unit_ready[u] = (projected[u], *rows_sent)

    def values(u):
        b, g = divmod(u, NG)
        s = u % 2
        for half in range(2):
            i, bank, free = prj_bank()
            for n in range(2):
                t = m.matmul(bank[:, n * G * E:(n + 1) * G * E], XT[:, (2 * half + n) * P:(2 * half + n + 1) * P],
                             W[:, 2, G * g:G * g + G, :], t_w[2], xT_ready[b], free, signal=n == 1)
            xT_used[b] = t
            src = bank.rearrange("p (n g e) -> p n g e", n=2, g=G)
            bias = bv[:, G * g:G * g + G, :].unsqueeze(1).broadcast_to([P, 2, G, E])
            t = m.tensor_op(m.dve, V[:, s, 2 * half:2 * half + 2, :, :], src, bias, ALU.add, t, t_rest, pv_done.get(u - 2))
            prj_free[i] = t
        values_ready[u] = t

    def distances(u, h, between):
        s = u % 2
        for half in range(2):
            i = turn["score"]
            turn["score"] = 1 - i
            ps = score_ps[i]
            for n in range(2):
                sl = 2 * half + n
                t = m.matmul(ps[:, n, :], KA[:, s, h, sl * P:(sl + 1) * P], QA[:, s, h, :], *unit_ready[u],
                             score_free[i], signal=n == 1)
            v = m.scalar_op(m.dve, S[:, s, h, 2 * half:2 * half + 2, :], ps[:, :, :], 0.0, None, ALU.max, None,
                            t, S_used[s])
            score_free[i] = v
            scored[u] = t
            if half == 0 and between:
                between.popleft()()
        flat = S[:, s, h, :, :].rearrange("p n t -> p (n t)")
        d2_done[u, h] = m.activate(flat, flat, ACT.Sqrt, v, bias=k["eps"][:, 2:3])
        if between:
            between.popleft()()

    def weights(u, h):
        s = u % 2
        flat = S[:, s, h, :, :].rearrange("p n t -> p (n t)")
        t = m.activate(flat, flat, ACT.Ln, d2_done[u, h], k["ready"], bias=k["eps"][:, 0:1])
        w_done[u, h] = m.activate(flat, flat, ACT.Exp, t, scale=-2.0, bias=k["eps"][:, 2:3])

    def sum_tiles(u, h):
        s = u % 2
        m.tensor_op(m.pool, W2[:, :, :], S[:, s, h, 0:2, :], S[:, s, h, 2:4, :], ALU.add, w_done[u, h])
        ws_done[u, h] = m.tensor_op(m.pool, WS[:, h, :], W2[:, 0, :], W2[:, 1, :], ALU.add, ws_used[h])

    def apply_pair(u, pr):
        b, g = divmod(u, NG)
        s = u % 2
        values, sums = pv_ps[:, 0, :], pv_ps[:, 1, :]
        rows = [slice(0, E), slice(E, P)]
        heads = (2 * pr, 2 * pr + 1)
        for n in range(NT):
            for odd, h in enumerate(heads):
                t = m.matmul(values[rows[odd], :], V[:, s, n, h, :], S[:, s, h, n, :], w_done[u, h], values_ready[u],
                             pv_free[0], start=n == 0, stop=n == NT - 1, signal=n == NT - 1)
        pv_done[u] = t
        for odd, h in enumerate(heads):
            c = m.matmul(sums[rows[odd], :], k["ones"][:, 0:E], WS[:, h, :], ws_done[u, h], pv_free[1])
            ws_used[h] = c
        S_used[s] = c
        v = m.tensor_op(m.dve, HT[:, 2 * g + pr, :], values, GT[:, u % 3, pr, :], ALU.mult, t, gate_ready[u, pr],
                        ht_used[0])
        gt_used[u] = pv_free[0] = v
        to_divide[u, pr] = (v, c)

    def divide_pair(u, pr):
        v, c = to_divide[u, pr]
        a = m.activate(RR[:, pr, :], pv_ps[:, 1, :], ACT.Ln, c, rr_used[pr], bias=k["eps"][:, 0:1])
        pv_free[1] = a
        inverse[u, pr] = m.activate(RR[:, pr, :], RR[:, pr, :], ACT.Exp, a, scale=-1.0, bias=k["eps"][:, 2:3])

    def normalise_pair(u, pr):
        ht = HT[:, 2 * (u % NG) + pr, :]
        rr_used[pr] = ht_ready[0] = m.tensor_op(m.dve, ht, ht, RR[:, pr, :], ALU.mult, inverse[u, pr],
                                                to_divide[u, pr][0])

    to_divide, gate_ready, inverse = {}, {}, {}
    rr_used, ht_ready, ws_used, ws_done = [None, None], [None], [None] * G, {}

    def finish_batch(b):
        Y = X[:, b % 2]
        for n in range(NT):
            t_xb = m.tensor_op(m.pool, Y[:, n, :], Y[:, n, :], bo[:, :], ALU.add, t_rest, t_x[b % 2], xT_ready[b])
        i, bank, free = prj_bank()
        for n in range(NT):
            for q in range(H // 2):
                t = m.matmul(bank[:, n * P:(n + 1) * P], HT[:, q, n * P:(n + 1) * P], Wo[:, q, :], t_rest, ht_ready[0], free,
                             start=q == 0, stop=q == H // 2 - 1, signal=q == H // 2 - 1 and n == NT - 1)
        ht_used[0] = t
        v = m.tensor_op(m.dve, Y, bank.rearrange("p (n c) -> p n c", n=NT), Y, ALU.add, t, t_xb)
        prj_free[i] = v
        moments[0] = row_moments(m, Y, tmp, NT, v)

    def normalise_batch(b):
        o = x1[:, b * NT:(b + 1) * NT, :]
        r = x_used[b] = normalise_rows(m, X[:, b % 2], o, tmp, NT, inverse_deviation(m, tmp, NT, moments[0]))
        load_x(b + 2)
        rows = slice(b * T, (b + 1) * T)
        m.sp.dma(out_lane[0], m.x1_dram[rows, :].rearrange("(n p) d -> p n d", p=P), o, r)
        m.sp.dma(out_lane[1], m.acc_dram[0][rows, :].rearrange("(n p) d -> p n d", p=P), o, r)

    moments = [None]

    units = B * NG
    load_x(1)
    transpose_x(0)
    project_pair(0, 0)
    project_pair(0, 1)
    square_rows(0)
    values(0)
    for u in range(units + 2):
        if 0 < u < NACC:
            m.zero_accumulator(u)
        now, before, after = u < units, 0 < u <= units, u + 1 < units
        ended = u - 2 if u >= 2 and (u - 2) % NG == NG - 1 else None
        between = deque()
        if after:
            if (u + 1) % NG == 0:
                between.append(lambda: transpose_x((u + 1) // NG))
            for pr in range(2):
                for part in (0, 1, 3):
                    between.append(lambda pr=pr, part=part: project_pair(u + 1, pr, (part,)))
        if u >= 2:
            between.insert(min(1, len(between)), lambda: normalise_pair(u - 2, 1))
        if before:
            for h in range(G):
                sum_tiles(u - 1, h)
        if now:
            for h in range(G):
                distances(u, h, between)
            m.load_table("natural_log_exp_and_others")
        while between:
            between.popleft()()
        if ended is not None:
            finish_batch(ended // NG)
        if now:
            weights(u, 0)
        if before:
            apply_pair(u - 1, 0)
            divide_pair(u - 1, 0)
        if after:
            square_rows(u + 1)
        if now:
            weights(u, 1)
        if ended is not None:
            normalise_batch(ended // NG)
        if before:
            apply_pair(u - 1, 1)
            divide_pair(u - 1, 1)
            normalise_pair(u - 1, 0)
        if after:
            values(u + 1)
        if now:
            weights(u, 2)
            weights(u, 3)
    m.x1_stored = [(l.sem, l.total) for l in out_lane]


def route(m, d, x1, meanwhile):
    E, D = d["Wr"].shape
    T = x1.shape[1] * P
    C = int(1.5 * T / E)
    HALF = T // 2
    k, sb = m.k, m.stage_sb
    assert C == P
    x1T = sb("r_x1T", [P, T])
    Wr = sb("r_Wr", [E, D])
    WrT = sb("r_WrT", [P, 64])
    L = sb("r_L", [P, HALF])
    vals = sb("r_vals", [P, C])
    idx = sb("r_idx", [P, C], U32)
    idxf = sb("r_idxf", [P, C])
    off = sb("r_off", [P, 1])
    vT, iT = sb("r_vT", [P, P]), sb("r_iT", [P, P])
    vB, iB = sb("r_vB", [P, E]), sb("r_iB", [P, E])
    ge, dif, best = sb("r_ge", [P, E]), sb("r_dif", [P, E]), sb("r_best", [P, E])
    pick = sb("r_pick", [P, E])
    rows, mx, ex, sm, rs = (sb("r_rows", [E, C]), sb("r_mx", [E, 1]), sb("r_ex", [E, C]), sb("r_sm", [E, 1]),
                            sb("r_rs", [E, 1]))
    ps = m.ps
    mirror = sb("r_mirror", [P, P])
    m.memset(m.pool, mirror[:, :], 0.0)
    t_mirror = m.pool.do(lambda e: e.affine_select(out=mirror[:, :], in_=mirror[:, :], compare_op=ALU.not_equal,
                                                   fill=1.0, base=1 - P, pattern=[[1, P]], channel_multiplier=1))
    lane = m.lane("r_l")
    t_in = m.sp.dma(lane, Wr[:, :], d["Wr"])
    meanwhile()
    z = m.memset(m.dve, WrT[:, :], 0.0)
    m.memset(m.dve, off[0:64, :], 0.0)
    t_off = m.memset(m.dve, off[64:P, :], float(HALF))
    x1T_ready, free = [], [None, None]
    for q in range(T // 512):
        bank = ps[0][:, q % 2, :]
        for n in range(4):
            t = m.transpose(bank[:, n * P:(n + 1) * P], x1[:, 4 * q + n, :], k["ident"][:, :], free[q % 2],
                            signal=n == 3)
        here = x1T[:, q * 512:(q + 1) * 512]
        free[q % 2] = m.activate(here, bank, ACT.Copy, t) if q % 2 else m.copy(m.dve, here, bank, t)
        x1T_ready.append(free[q % 2])
    t = m.transpose(ps[3][:, 0, 0:E], Wr[:, :], k["ident"][0:E, 0:E], t_in)
    w = m.copy(m.dve, WrT[:, 0:E], ps[3][:, 0, 0:E], t, z)
    for c in range(HALF // 512):
        out = ps[1 + c // 2][:, c % 2, :]
        m.matmul(out[0:64, :], WrT[:, :], x1T[:, c * 512:(c + 1) * 512], w, *x1T_ready[-2:])
        t = m.matmul(out[64:P, :], WrT[:, :], x1T[:, HALF + c * 512:HALF + (c + 1) * 512])
        last = m.copy(m.dve, L[:, c * 512:(c + 1) * 512], out, t)
    for r in range(C // 8):
        eight = slice(8 * r, 8 * r + 8)
        t = m.dve.do(lambda e, s=eight: e.max(vals[:, s], L[:, :]), last)
        t = m.dve.do(lambda e, s=eight: e.max_index(idx[:, s], vals[:, s], L[:, :]), t)
        if r < C // 8 - 1:
            t = m.dve.do(lambda e, s=eight: e.match_replace(L[:, :], vals[:, s], L[:, :], -3.0e38), t)
        last = t
    t = m.copy(m.dve, idxf[:, :], idx[:, :], last)
    t = m.scalar_op(m.dve, idxf[:, :], idxf[:, :], off[:, 0:1], None, ALU.add, None, t, t_off)
    m.transpose(ps[0][:, 0, 0:P], vals[:, :], k["ident"][:, :], t)
    t = m.transpose(ps[0][:, 0, P:2 * P], idxf[:, :], k["ident"][:, :])
    m.copy(m.dve, vT[:, :], ps[0][:, 0, 0:P], t)
    t = m.copy(m.dve, iT[:, :], ps[0][:, 0, P:2 * P])
    m.matmul(ps[3][:, 0, 0:E], mirror[:, :], vT[:, 64:64 + E], t, t_mirror)
    t = m.matmul(ps[3][:, 0, 64:64 + E], mirror[:, :], iT[:, 64:64 + E])
    m.copy(m.dve, vB[:, :], ps[3][:, 0, 0:E], t)
    t = m.copy(m.dve, iB[:, :], ps[3][:, 0, 64:64 + E])
    m.tensor_op(m.dve, ge[:, :], vT[:, 0:E], vB[:, :], ALU.is_ge, t)
    m.tensor_op(m.dve, best[:, :], vT[:, 0:E], vB[:, :], ALU.max)
    t = m.tensor_op(m.dve, dif[:, :], iT[:, 0:E], iB[:, :], ALU.subtract)
    t = m.tensor_op(m.dve, dif[:, :], dif[:, :], ge[:, :], ALU.mult, t)
    t = m.tensor_op(m.dve, pick[:, :], dif[:, :], iB[:, :], ALU.add, t)
    m.routed = m.copy(m.dve, m.token[:, :], pick[:, :], t)
    t = m.transpose(ps[0][0:E, 1, 0:C], best[:, :], k["ident"][:, :], m.routed)
    a = m.copy(m.dve, rows[:, :], ps[0][0:E, 1, 0:C], t)
    t = m.dve.do(lambda e: e.tensor_reduce(mx[:, :], rows[:, :], AX_X, ALU.max), a)
    t = m.scalar_op(m.dve, rows[:, :], rows[:, :], mx[:, 0:1], None, ALU.subtract, None, t)
    t = m.activate(ex[:, :], rows[:, :], ACT.Exp, t, bias=k["eps"][0:E, 2:3], accum_out=sm[:, 0:1])
    t = m.dve.do(lambda e: e.reciprocal(rs[:, :], sm[:, :]), t)
    t = m.scalar_op(m.dve, ex[:, :], ex[:, :], rs[:, 0:1], None, ALU.mult, None, t)
    t = m.transpose(ps[3][:, 1, 0:E], ex[:, :], k["ident"][0:E, 0:E], t)
    m.share_ready = m.copy(m.dve, m.share[:, :], ps[3][:, 1, 0:E], t)


NACC = 4


def experts(m, d, beside):
    E, NS, D, M = d["W1"].shape
    K = d["W2"].shape[3]
    k, sb = m.k, m.stage_sb
    NB = 8
    xg = sb("e_xg", [P, NB, D])
    xgT = sb("e_xgT", [P, NB, P])
    W1 = sb("e_W1", [P, NB, NS, M])
    W2 = sb("e_W2", [P, NB, NS, K])
    b2r, b2T = sb("e_b2r", [E, NS * K]), sb("e_b2T", [P, E])
    yT = sb("e_yT", [P, 2, P])
    b1r = sb("e_b1r", [P, 2, M])
    b1T = sb("e_b1T", [P, E * NS])
    hT = sb("e_hT", [P, NB, NS, P])
    y = sb("e_y", [P, NACC, NS * K])
    l_b1 = m.lane("e_l_b1")
    l_w = [m.lane(f"e_l_w{i}") for i in range(NB)]
    l_g = [m.lane(f"e_l_g{i}") for i in range(NB)]
    l_s = [m.lane(f"e_l_s{i}") for i in range(NACC)]
    half = E * NS // 2
    t_b1 = m.sp.dma(l_b1, b1r[0:half, :, :], d["b1"].rearrange("e s m -> (e s) m").rearrange("(a r) m -> r a m", a=2))
    t_b2 = m.sp.dma(m.lane("e_l_b2"), b2r[:, :], d["b2"].rearrange("e s k -> e (s k)"))
    t_w, t_g = {}, {}
    xg_used, w_used, y_sent = {}, {}, {}

    def load_weights(e):
        i = e % NB
        m.sp.wait(w_used.get(e - NB))
        m.sp.dma(l_w[i], W1[:, i, :, :], d["W1"][e].rearrange("s d m -> d s m"))
        t_w[e] = m.sp.dma(l_w[i], W2[:, i, :, :], d["W2"][e].rearrange("s m k -> m s k"))

    def gather(e):
        i = e % NB
        m.pool.wait(m.routed, *m.x1_stored, xg_used.get(e - NB))
        lane = l_g[i]
        lane.total += 16
        m.pool.queue.append(lambda g, e=e, i=i, lane=lane: g.indirect_dma_start(
            xg[:, i, :], None, m.x1_dram[:, :], bass.IndirectOffsetOnAxis(m.token[:, e:e + 1], 0)).then_inc(lane.sem, 16))
        t_g[e] = (lane.sem, lane.total)

    evac = {}
    ps_free = {}

    def transpose_in(e):
        i = e % NB
        bank = m.ps[0][:, e % 2, 0:P]
        t = m.transpose(bank, xg[:, i, :], k["ident"][:, :], t_g[e], ps_free.get(("x", e % 2)), t_b1T, t_b2T)
        xg_used[e] = t
        v = m.copy(m.dve, xgT[:, i, :], bank, t, w_used.get(e - NB))
        ps_free["x", e % 2] = v
        evac[e] = v

    def hidden(e):
        i = e % NB
        bank = m.ps[1][:, e % 2, :]
        for s in range(NS):
            t = m.matmul(bank[:, s * P:(s + 1) * P], W1[:, i, s, :], xgT[:, i, :], t_w[e], evac[e],
                         ps_free.get(("h", e % 2)), signal=s == NS - 1)
        for s in range(NS):
            a = m.activate(hT[:, i, s, :], bank[:, s * P:(s + 1) * P], ACT.Gelu, t, t_b1T, w_used.get(e - NB),
                           bias=b1T[:, e * NS + s:e * NS + s + 1])
        ps_free["h", e % 2] = a
        return a

    def output(e, a):
        i = e % NB
        bank = m.ps[2][:, e % 2, 0:P]
        for s in range(NS):
            t = m.matmul(bank[s * K:(s + 1) * K, :], W2[:, i, s, :], hT[:, i, s, :], a, t_w[e], ps_free.get(("y", e % 2)))
        w_used[e] = t
        yT_ready[e] = ps_free["y", e % 2] = m.scalar_op(m.dve, yT[:, e % 2, :], bank, b2T[:, e:e + 1], None, ALU.add, None,
                                                        t, t_b2T, yT_used.get(e - 2))

    yT_ready, yT_used = {}, {}

    def scatter(e):
        j = e % NACC
        bank = m.ps[3][:, 0, 0:P]
        yT_used[e] = t = m.transpose(bank, yT[:, e % 2, :], k["ident"][:, :], yT_ready[e], m.turn_free)
        v = m.scalar_op(m.dve, y[:, j, :], bank, m.share[:, e:e + 1], None, ALU.mult, None, t, m.share_ready,
                        y_sent.get(e - NACC))
        m.turn_free = v
        lane = l_s[j]
        m.pool.wait(v, y_sent.get(e - NACC), *m.x1_stored, m.zeroed)
        lane.total += 16
        m.pool.queue.append(lambda g, e=e, j=j, lane=lane: g.indirect_dma_start(
            m.acc_dram[j][:, :], bass.IndirectOffsetOnAxis(m.token[:, e:e + 1], 0), y[:, j, :], None,
            compute_op=ALU.add).then_inc(lane.sem, 16))
        y_sent[e] = (lane.sem, lane.total)

    act_done = {}
    for e in range(NB - 1):
        load_weights(e)
    yield
    m.turn_free = m.share_ready
    for e in range(NB - 1):
        gather(e)
    for a in range(2):
        t = m.transpose(m.ps[0][:, 0, a * half:(a + 1) * half], b1r[0:half, a, :], k["ident"][0:half, 0:half], t_b1,
                        m.share_ready)
    t_b1T = m.copy(m.dve, b1T[:, :], m.ps[0][:, 0, 0:E * NS], t)
    t = m.transpose(m.ps[0][:, 1, 0:E], b2r[:, :], k["ident"][0:E, 0:E], t_b2)
    t_b2T = m.copy(m.dve, b2T[:, :], m.ps[0][:, 1, 0:E], t)
    transpose_in(0)
    for e in range(E + 2):
        if e + 1 < E:
            transpose_in(e + 1)
        if e < E:
            act_done[e] = hidden(e)
        if e > 1:
            scatter(e - 2)
        if 0 < e <= E:
            output(e - 1, act_done[e - 1])
        if e + NB - 1 < E:
            load_weights(e + NB - 1)
            gather(e + NB - 1)
        if e == NB:
            beside()
    m.scattered = [y_sent[e] for e in range(E - NACC, E)]
    yield


class Joiner:

    def __init__(self, m, x2):
        self.m, self.x2 = m, x2
        sb = m.stage_sb
        self.A = sb("j_A", [P, 1, NACC, 4, P])
        self.tmp = ln_buffers(sb, "j_ln", 4)
        self.lane = m.lane("j_l")
        self.used, self.ready = None, {}
        self.borrowed = {}

    def steps(self, b, x2_free=None):
        m, NT = self.m, 4
        a = self.A[:, 0]
        m.sp.wait(*m.scattered, self.used, *self.borrowed.values())
        for j in range(NACC):
            t = m.sp.dma(self.lane, a[:, j], m.acc_dram[j][b * NT * P:(b + 1) * NT * P, :]
                         .rearrange("(n p) d -> p n d", p=P))
        yield
        u = m.tensor_op(m.dve, a[:, 0], a[:, 0], a[:, 1], ALU.add, t)
        v = m.tensor_op(m.dve, a[:, 2], a[:, 2], a[:, 3], ALU.add)
        t = m.tensor_op(m.dve, a[:, 0], a[:, 0], a[:, 2], ALU.add, u, v)
        t = row_moments(m, a[:, 0], self.tmp, NT, t)
        yield
        t = inverse_deviation(m, self.tmp, NT, t)
        yield
        self.used = self.ready[b] = normalise_rows(m, a[:, 0], self.x2[:, b % 3], self.tmp, NT, t, x2_free)

def relative_attention(m, d, dffn, out, x1):
    B, T, D, H = 8, 512, 128, 16
    DH = D // H
    NT = T // P
    HB = H // 2
    SCALE = float(DH) ** -0.5
    LEFT = [(0, 0, 3), (1, 3, 2), (2, 5, 1)]
    RIGHT = [(0, 0), (1, 1), (2, 2), (0, 3), (1, 4), (0, 5)]
    ROWS = 6 * DH
    BF16 = mybir.dt.bfloat16
    k, sb = m.k, m.stage_sb
    Wq, Wk, Wp, Wv, Wo = (sb("c_" + n, [P, D]) for n in ("Wq", "Wk", "Wp", "Wv", "Wo"))
    rows = sb("c_rows", [1, 6, D])
    cols = sb("c_cols", [P, 6])
    bv, bo = sb("c_bv", [P, D]), sb("c_bo", [P, D])
    peT = sb("c_peT", [P, T])
    PART = sb("c_PART", [P, 3, 3, T], BF16)
    RES = sb("c_RES", [P, 3, T])
    QU = sb("c_QU", [P, 2, HB, T], BF16)
    QV = sb("c_QV", [P, 2, HB, T], BF16)
    KR = sb("c_KR", [P, 2, HB // 2, T], BF16)
    PR = sb("c_PR", [P, H // 2, T], BF16)
    V = sb("c_V", [P, 2, NT, H, 32])
    fold = sb("c_fold", [P, DH + 1])
    ffn = GatedLayers(m, dffn, out)
    u_ps = [m.ps[0][:, 0, :], m.ps[0][:, 1, :]]
    c_ps = [m.ps[1][:, 0, :], m.ps[1][:, 1, :]]
    t_ps = m.ps[2]
    o_ps, j_ps = m.ps[3][:, 0, :], m.ps[3][:, 1, :]
    n_view = j_ps[:, 0:NT * (DH + 1)].rearrange("p (n c) -> p n c", n=NT)

    l_in = m.lane("c_l_in")
    for tile, name in ((Wq, "Wq"), (Wk, "Wk"), (Wp, "Wp"), (Wv, "Wv"), (Wo, "Wo")):
        m.sp.dma(l_in, tile[:, :], d[name])
    for n, name in enumerate(("bq", "bk", None, None, "ln_g", "ln_b")):
        if name:
            m.sp.dma(l_in, rows[:, n, :], d[name].rearrange("(a e) -> a e", a=1))
    m.sp.dma(l_in, rows[:, 2, :], d["u_bias"].rearrange("(a h) e -> a (h e)", a=1))
    m.sp.dma(l_in, rows[:, 3, :], d["v_bias"].rearrange("(a h) e -> a (h e)", a=1))
    m.sp.dma(l_in, bv[:, :], d["bv"].rearrange("(a e) -> a e", a=1).broadcast_to([P, D]))
    m.sp.dma(l_in, bo[:, :], d["bo"].rearrange("(a e) -> a e", a=1).broadcast_to([P, D]))
    t_in = m.sp.dma(l_in, peT[:, :], d["peT"])

    m.memset(m.pool, QU[:, :, :, :], 0.0)
    m.memset(m.pool, QV[:, :, :, :], 0.0)
    m.memset(m.pool, KR[:, :, :, :], 0.0)
    m.memset(m.pool, PR[:, :, :], 0.0)
    m.memset(m.pool, V[:, :, :, :, DH + 1:32], 0.0)
    m.memset(m.pool, V[:, :, :, :, DH:DH + 1], 1.0)
    m.memset(m.pool, fold[:, :], 0.0)
    for q in range(4):
        z = m.pool.do(lambda e, q=q: e.affine_select(
            out=fold[:, :], in_=fold[:, :], compare_op=ALU.not_equal, fill=1.0, base=-32 * q,
            pattern=[[-1, DH + 1]], channel_multiplier=1))

    yield
    m.tensor_op(m.dve, rows[:, 2, :], rows[:, 0, :], rows[:, 2, :], ALU.add, t_in)
    t = m.tensor_op(m.dve, rows[:, 3, :], rows[:, 0, :], rows[:, 3, :], ALU.add)
    for n, src in enumerate((2, 3, 1, 4, 5)):
        c = m.matmul(j_ps[:, n:n + 1], rows[:, src, :], k["ones"][0:1, 0:1], t, m.share_ready)
    cols_ready = m.copy(m.dve, cols[:, 0:5], j_ps[:, 0:5], c)
    ffn.turn_weights(o_ps)
    st = {"j": cols_ready, "t": None, "u": [None, None], "c": [None, None], "o": None, "ot": None}
    stack_lane = m.lane("c_l_parts")
    stack_used = {}

    def split_high(bank, t, *tensors):
        for n, bias in tensors:
            hi = m.activate(PART[:, n, 0, :], bank, ACT.Identity, t, cols_ready, part_sent[n], bias=bias)
        for n, bias in tensors:
            m.dve.wait(hi, split_used[n])
            left[n] = m.dve.do(lambda e, n=n, bias=bias: e.scalar_tensor_tensor(RES[:, n, :], bank, bias, PART[:, n, 0, :],
                                                                                ALU.add, ALU.subtract), t)
        return left[n]

    def split_middle(n):
        middle[n] = m.activate(PART[:, n, 1, :], RES[:, n, :], ACT.Copy, left[n])

    def split_low(n):
        low[n] = split_used[n] = m.tensor_op(m.dve, PART[:, n, 2, :], RES[:, n, :], PART[:, n, 1, :], ALU.subtract,
                                             middle[n])

    left, middle, low, split_used, part_sent = ([None] * 3 for _ in range(5))

    def stack_rows(n):
        return m.stack_dram[n].rearrange("(h j e) t -> j h e t", j=6, e=DH)

    def send_parts(n):
        for j, part in enumerate((0, 1, 2, 0, 1, 0) if n == 2 else (0, 0, 0, 1, 1, 2)):
            part_sent[n] = m.sp.dma(stack_lane, stack_rows(n)[j], PART[:, n, part, :], low[n], sent_read[0])
        return part_sent[n]

    def stack_half(n, half, odd):
        v = m.stack_dram[n].rearrange("(q o r) t -> o r q t", o=2, r=ROWS)[odd]
        return v[:, half * (HB // 2):(half + 1) * (HB // 2), :]

    t = m.matmul(j_ps, Wp[:, :], peT[:, :], t_in, st["j"])
    m.memset(m.dve, cols[:, 5:6], 0.0)
    m.act.wait((m.dve.sem, m.dve.count))
    m.dve.wait((m.dve.sem, m.dve.count))
    st["j"] = split_high(j_ps, t, (2, cols[:, 5:6]))
    split_middle(2)
    split_low(2)
    sent_read = [None]
    t = send_parts(2)
    for odd in range(2):
        v = m.stack_dram[2].rearrange("(q o r) t -> o r q t", o=2, r=ROWS)[odd]
        t = m.sp.dma(stack_lane, PR[64 * odd:64 * odd + ROWS, :, :], v, t, z)
        pr_loaded = t
    sent_read[0] = t
    yield

    sb = m.stage_sb
    x2 = sb("c_x2", [P, 3, NT, D])
    joiner = Joiner(m, x2)
    XN = joiner.A[:, 0, 1]
    XNT = joiner.A[:, 0, 2].rearrange("p n d -> p (n d)")
    HDT = joiner.A[:, 0, 3].rearrange("p n d -> p (n d)")
    NU, NK = 2, 4
    U = sb("c_U", [P, NU, NT, T + 1])
    SK = sb("c_SK", [P, NK, NT, T])
    TS = x1.rearrange("p (s n r) d -> p s n (r d)", s=2, n=NT)
    MX = sb("c_MX", [P, 2, NT])
    EX = sb("c_EX", [P, 2, NT, T])
    OT = sb("c_OT", [P, T])
    RS = sb("c_RS", [P, NT])
    HD = sb("c_HD", [P, 2, NT, H, DH])
    Y = sb("c_Y", [P, NT, D])
    tmp = ln_buffers(sb, "c_ln", NT)
    tmp2 = ln_buffers(sb, "c_ln2", NT)
    ffn.place_buffers()
    z = m.memset(m.pool, U[:, :, :, 0:1], 0.0)

    l_store = [m.lane(f"c_l_store{i}") for i in range(NU)]
    l_fetch = [m.lane(f"c_l_fetch{i}") for i in range(NK)]
    l_stack = [m.lane(f"c_l_stack{i}") for i in range(2)]
    stored, fetched, sk_used = {}, {}, {}
    ts_ready, ts_used, ex_ready, pv_done, hd_used = {}, {}, {}, {}, [None, None]
    stacks, sent, v_ready, users = {}, {}, {}, {}

    def prepare(b):
        x = x2[:, b % 3]
        t = row_moments(m, x, tmp, NT, joiner.ready[b])
        yield
        t = inverse_deviation(m, tmp, NT, t)
        yield
        r = normalise_rows(m, x, XN, tmp, NT, t, st.get("xn"))
        yield
        for n in range(NT):
            t = m.transpose(j_ps[:, n * P:(n + 1) * P], XN[:, n, :], k["ident"][:, :], r, st["j"], signal=n == NT - 1)
        st["xn"] = joiner.borrowed["xn"] = t
        st["j"] = xt = m.scalar_op(m.dve, XNT, j_ps, cols[:, 3:4], cols[:, 4:5], ALU.mult, ALU.add, t, cols_ready,
                                   st.get("xnt"))
        yield
        t = m.matmul(j_ps, Wq[:, :], XNT, xt, st["j"])
        st["j"] = split_high(j_ps, t, (0, cols[:, 0:1]), (1, cols[:, 1:2]))
        yield
        t = m.matmul(j_ps, Wk[:, :], XNT, xt, st["j"])
        st["j"] = split_high(j_ps, t, (2, cols[:, 2:3]))
        for n in range(2):
            split_middle(n)
        yield
        for n in range(2):
            split_low(n)
        split_middle(2)
        yield
        send_parts(0)
        send_parts(1)
        split_low(2)
        for n in range(NT):
            t = m.matmul(j_ps[:, n * P:(n + 1) * P], XNT[:, n * P:(n + 1) * P], Wv[:, :], st["j"], signal=n == NT - 1)
        st["xnt"] = joiner.borrowed["xnt"] = t
        st["j"] = v_ready[b] = m.tensor_op(
            m.dve, V[:, b % 2, :, :, 0:DH], j_ps.rearrange("p (n h e) -> p n h e", n=NT, h=H),
            bv[:, :].rearrange("p (h e) -> p h e", h=H).unsqueeze(1).broadcast_to([P, NT, H, DH]), ALU.add, t,
            users.get((b - 2, "pv")), z)
        yield
        sent[b] = send_parts(2)
        yield

    def load_stacks(c):
        b, half = divmod(c, 2)
        i = c % 2
        used = [stack_used.get((c - 2, kind)) for kind in ("pos", "content")]
        for odd in range(2):
            rs = slice(64 * odd, 64 * odd + ROWS)
            for tile, n, step in ((QV, 1, 2), (QU, 0, 2), (KR, 2, 1)):
                dst = tile[rs, i, odd:HB:2, :] if step == 2 else tile[rs, i, :, :]
                t = m.sp.dma(l_stack[i], dst, stack_half(n, half, odd), sent[b], z, *used)
        stacks[c] = t
        if half:
            sent_read[0] = t

    def positions(w, n):
        b, h = divmod(w, H)
        c, g = w // HB, h % HB
        i, j2, j = w % NU, w % NK, n % 2
        t = m.matmul(u_ps[j], QV[:, c % 2, g, n * P:(n + 1) * P], PR[:, h // 2, :], stacks[c], pr_loaded, st["u"][j])
        a = st["u"][j] = m.activate(U[:, i, n, 1:T + 1], u_ps[j], ACT.Copy, t, z, stored.get(w - NU))
        if n == NT - 1:
            stack_used[c, "pos"] = t
        if n % 2:
            two = slice(n - 1, n + 1)
            stored[w] = m.act.dma(l_store[i], m.shift_dram[j2].rearrange("(n p) c -> p n c", p=P)[:, two, :],
                                 U[:, i, two, :], a, fetched.get(w - NK))

    def fetch(w):
        j2 = w % NK
        flat = m.shift_dram[j2].rearrange("a c -> (a c)")[T:T + T * T]
        fetched[w] = m.sp.dma(l_fetch[j2], SK[:, j2, :, :], flat.rearrange("(n p c) -> p n c", p=P, c=T), stored[w],
                              sk_used.get(w - NK))

    def scores(w, n):
        b, h = divmod(w, H)
        c, g = w // HB, h % HB
        i, s, j = w % NK, w % 2, n % 2
        t = m.matmul(c_ps[j], QU[:, c % 2, g, n * P:(n + 1) * P], KR[:, c % 2, g // 2, :], stacks[c], st["c"][j])
        m.dve.wait(t, fetched[w], ts_used.get(w - 2))
        v = st["c"][j] = m.dve.do(lambda e: e.tensor_tensor_reduce(
            TS[:, s, n, :], c_ps[j], SK[:, i, n, :], 1.0, -3.0e38, ALU.add, ALU.max, MX[:, s, n:n + 1]))
        stack_used[c, "content"] = t
        sk_used[w] = v
        if n == 0:
            first_less[w] = m.scalar_op(m.pool, TS[:, s, 0, :], TS[:, s, 0, :], MX[:, s, 0:1], None, ALU.subtract, None, v)

    def less_max(w):
        s = w % 2
        for n in range(1, NT):
            v = m.scalar_op(m.dve, TS[:, s, n, :], TS[:, s, n, :], MX[:, s, n:n + 1], None, ALU.subtract, None,
                            sk_used[w])
        ts_ready[w] = (first_less[w], v)

    first_less = {}

    def turn_exp(w, half):
        s = w % 2
        for c in range(2):
            jb = 2 * half + c
            for n in range(NT):
                t = m.transpose(t_ps[:, c, n * P:(n + 1) * P], TS[:, s, n, jb * P:(jb + 1) * P], k["ident"][:, :],
                                *ts_ready[w], st["t"], signal=n == NT - 1)
        a = m.activate(EX[:, s, 2 * half:2 * half + 2, :], t_ps[:, :, :], ACT.Exp, t, pv_done.get(w - 2),
                       scale=SCALE, bias=k["eps"][:, 2:3])
        st["t"] = a
        ts_used[w] = t
        ex_ready[w] = a

    def apply(w):
        b, h = divmod(w, H)
        for jb in range(NT):
            t = m.matmul(o_ps[32 * jb:32 * jb + 32, :], V[:, b % 2, jb, h, :], EX[:, w % 2, jb, :], ex_ready[w],
                         v_ready[b], st["o"])
        pv_done[w] = users[b, "pv"] = t
        ot_ready[w] = st["o"] = m.copy(m.dve, OT[:, :], o_ps, t, st["ot"])

    def fold_apply(w):
        b, h = divmod(w, H)
        for n in range(NT):
            t = m.matmul(n_view[:, n, :], OT[:, n * P:(n + 1) * P], fold[:, :], ot_ready[w], st["j"])
        st["ot"] = t
        v = m.dve.do(lambda e: e.reciprocal(RS[:, :], n_view[:, :, DH]), t)
        t = m.tensor_op(m.dve, HD[:, b % 2, :, h, :], n_view[:, :, 0:DH], RS[:, :].unsqueeze(2).broadcast_to([P, NT, DH]),
                        ALU.mult, v, hd_used[b % 2])
        st["j"] = t
        if h == H - 1:
            endings.append(finish(b, t))

    ot_ready = {}

    def finish(b, hd_ready):
        x = x2[:, b % 3]
        for n in range(NT):
            xb = m.tensor_op(m.pool, Y[:, n, :], x[:, n, :], bo[:, :], ALU.add, joiner.ready[b], t_in, st.get("y"))
            t = m.transpose(j_ps[:, n * P:(n + 1) * P], HD[:, b % 2, n, :, :].rearrange("p h e -> p (h e)"),
                            k["ident"][:, :], hd_ready, st["j"], signal=n == NT - 1)
        x2_used[b] = xb
        hd_used[b % 2] = t
        st["j"] = v = m.copy(m.dve, HDT, j_ps, t, st.get("hdt"))
        yield
        for n in range(NT):
            t = m.matmul(j_ps[:, n * P:(n + 1) * P], HDT[:, n * P:(n + 1) * P], Wo[:, :], v, st["j"])
        st["hdt"] = joiner.borrowed["hdt"] = t
        st["j"] = v = m.tensor_op(m.dve, Y[:, :, :], j_ps.rearrange("p (n c) -> p n c", n=NT), Y[:, :, :],
                                  ALU.add, t, xb)
        t = row_moments(m, Y, tmp2, NT, v)
        yield
        t = inverse_deviation(m, tmp2, NT, t)
        yield
        st["y"] = normalise_rows(m, Y, ffn.x3, tmp2, NT, t, ffn.x3_used)
        yield
        yield from ffn.steps(b, st, j_ps, st["y"])

    x2_used = {}
    beginnings, endings = deque(), deque()

    def run_piece(tasks):
        while tasks:
            if next(tasks[0], "end") != "end":
                return
            tasks.popleft()

    W = B * H
    LEAD = 4
    m.load_table("natural_log_exp_and_others")
    beginnings.extend([joiner.steps(0), prepare(0)])
    while beginnings:
        run_piece(beginnings)
    load_stacks(0)
    joining = {1: joiner.steps(1)}
    next(joining[1])
    for step in range(W + LEAD + 3):
        new, now, turned, applied = step, step - LEAD, step - LEAD - 1, step - LEAD - 2
        b = new // H
        if new < W and new % H == LEAD:
            load_stacks(2 * b + 1)
        if new % H == 0 and b + 1 < B:
            beginnings.extend([joining[b + 1], prepare(b + 1)])
        if new % H == H - 4 and b + 2 < B:
            joining[b + 2] = joiner.steps(b + 2, x2_used.get(b - 1))
            next(joining[b + 2])
        if new % H == H - 2 and b + 1 < B:
            while beginnings:
                run_piece(beginnings)
            load_stacks(2 * b + 2)
        if 0 < step <= W:
            fetch(step - 1)
        for half in range(2):
            for n in (2 * half, 2 * half + 1):
                if new < W:
                    positions(new, n)
                if 0 <= now < W:
                    scores(now, n)
            run_piece(endings if half else beginnings)
            if 0 <= turned < W:
                turn_exp(turned, half)
            if half == 0 and 0 <= applied < W:
                apply(applied)
        if 0 <= now < W:
            less_max(now)
        if 0 <= applied < W:
            fold_apply(applied)
    while endings:
        run_piece(endings)


class GatedLayers:

    def __init__(self, m, d, out):
        self.m, self.out = m, out
        D, E = d["gate_w"].shape
        self.D, self.E, self.NT = D, E, 4
        sb = m.stage_sb
        self.raw = raw = sb("f_raw", [P, 2, D])
        self.WT = sb("f_WT", [P, 2 * D + E])
        self.bb = sb("f_bb", [P, 2 * D])
        lane = m.lane("f_l")
        m.sp.dma(lane, raw[:, 0, :], d["w0"])
        m.sp.dma(lane, raw[:, 1, :], d["w1"])
        m.sp.dma(lane, self.WT[:, 2 * D:2 * D + E], d["gate_w"])
        m.sp.dma(lane, self.bb[:, 0:D], d["b0"].rearrange("(a e) -> a e", a=1).broadcast_to([P, D]))
        self.loaded = m.sp.dma(lane, self.bb[:, D:2 * D], d["b1"].rearrange("(a e) -> a e", a=1).broadcast_to([P, D]))

    def turn_weights(self, bank):
        m, D = self.m, self.D
        for n in range(2):
            t = m.transpose(bank[:, n * P:(n + 1) * P], self.raw[:, n, :], m.k["ident"][:, :], self.loaded, m.turn_free)
        m.turn_free = self.ready = m.copy(m.dve, self.WT[:, 0:2 * D], bank[:, 0:2 * D], t)

    def place_buffers(self):
        m, D, E, NT = self.m, self.D, self.E, self.NT
        sb = m.stage_sb
        self.x3, self.x3_used = sb("f_x3", [P, NT, D]), None
        self.XT = sb("f_XT", [P, NT, P])
        self.PRE = sb("f_PRE", [P, NT, 2 * D])
        self.LG, self.cmp = sb("f_LG", [P, NT, E]), sb("f_cmp", [P, NT, E])
        self.red, self.inv, self.rank, self.m0, self.m1 = (sb("f_" + n, [P, NT]) for n in
                                                            ("red", "inv", "rank", "m0", "m1"))
        self.coef = sb("f_coef", [P, 2, NT])
        self.Y = sb("f_Y", [P, NT, D])
        self.tmp = ln_buffers(sb, "f_ln", NT)
        self.l_out = m.lane("f_l_out")
        self.sent = self.lg_used = self.xt_used = None

    def steps(self, b, st, bank, x3_ready):
        m, D, E, NT, k = self.m, self.D, self.E, self.NT, self.m.k
        x3, LG, PRE, Y, coef, red, cmp = self.x3, self.LG, self.PRE, self.Y, self.coef, self.red, self.cmp
        for n in range(NT):
            t = m.transpose(bank[:, n * P:(n + 1) * P], x3[:, n, :], k["ident"][:, :], x3_ready, st["j"],
                            signal=n == NT - 1)
        st["j"] = xt = m.copy(m.dve, self.XT[:, :, :], bank.rearrange("p (n c) -> p n c", n=NT), t, self.xt_used)
        yield
        for n in range(NT):
            ps = bank[:, 0:2 * D + E]
            t = m.matmul(ps, self.XT[:, n, :], self.WT[:, :], xt, self.ready, st["j"])
            m.copy(m.dve, LG[:, n, :], ps[:, 2 * D:2 * D + E], t)
            st["j"] = pre = m.tensor_op(m.dve, PRE[:, n, :], ps[:, 0:2 * D], self.bb[:, :], ALU.add)
            yield
        self.xt_used = t

        def over_experts(col):
            return col.unsqueeze(2).broadcast_to([P, NT, E])

        t = m.dve.do(lambda e: e.tensor_reduce(red[:, :], LG[:, :, :], AX_X, ALU.max), pre)
        lg = m.tensor_op(m.dve, LG[:, :, :], LG[:, :, :], over_experts(red[:, :]), ALU.subtract, t)
        yield
        ex = m.activate(LG[:, :, :], LG[:, :, :], ACT.Exp, lg, bias=k["eps"][:, 2:3])
        yield
        a = m.activate(PRE[:, :, :], PRE[:, :, :], ACT.Silu, pre)
        m.load_table("natural_log_exp_and_others")
        yield
        t = m.dve.do(lambda e: e.tensor_reduce(red[:, :], LG[:, :, :], AX_X, ALU.add), ex)
        t = m.dve.do(lambda e: e.reciprocal(self.inv[:, :], red[:, :]), t)
        t = m.tensor_op(m.dve, LG[:, :, :], LG[:, :, :], over_experts(self.inv[:, :]), ALU.mult, t)
        r = m.dve.do(lambda e: e.tensor_reduce(red[:, :], LG[:, :, 1:E], AX_X, ALU.max), t)
        m.tensor_op(m.dve, cmp[:, :, 2:E], LG[:, :, 2:E], LG[:, :, 1:2].broadcast_to([P, NT, E - 2]), ALU.is_gt)
        t = m.tensor_op(m.dve, cmp[:, :, 1], LG[:, :, 0], LG[:, :, 1], ALU.is_ge)
        u = m.tensor_op(m.dve, self.m0[:, :], LG[:, :, 0], red[:, :], ALU.is_ge, r)
        t = m.dve.do(lambda e: e.tensor_reduce(self.rank[:, :], cmp[:, :, 1:E], AX_X, ALU.add), t)
        m.tensor_op(m.dve, coef[:, 0, :], LG[:, :, 0], self.m0[:, :], ALU.mult, u)
        t = m.scalar_op(m.dve, self.m1[:, :], self.rank[:, :], 1.0, None, ALU.is_equal, None, t)
        c = m.tensor_op(m.dve, coef[:, 1, :], LG[:, :, 1], self.m1[:, :], ALU.mult, t)
        yield
        for n in range(NT):
            t = m.scalar_op(m.dve, Y[:, n, :], PRE[:, n, 0:D], coef[:, 0, n:n + 1], None, ALU.mult, None, a, c,
                             self.sent)
        m.dve.wait(t)
        for n in range(NT):
            t = m.dve.do(lambda e, n=n: e.scalar_tensor_tensor(Y[:, n, :], PRE[:, n, D:2 * D], coef[:, 1, n:n + 1],
                                                              Y[:, n, :], ALU.mult, ALU.add))
        t = self.x3_used = m.tensor_op(m.dve, Y[:, :, :], Y[:, :, :], x3[:, :, :], ALU.add, t)
        t = row_moments(m, Y, self.tmp, NT, t)
        yield
        t = inverse_deviation(m, self.tmp, NT, t)
        yield
        r = normalise_rows(m, Y, Y, self.tmp, NT, t)
        self.sent = m.sp.dma(self.l_out, self.out[b].rearrange("(n p) d -> p n d", p=P), Y[:, :, :], r)
        m.final = self.sent
        yield


def two_layers_kernel(nc, ins, out):
    B, T, D = ins["L0_attn_X"].shape
    rows = B * T
    NTT = rows // P

    def part(prefix):
        return {n[len(prefix):]: ap for n, ap in ins.items() if n.startswith(prefix)}

    with ExitStack() as ctx:
        m = Machine(nc, ctx)
        m.ps = [ctx.enter_context(nc.psum_tensor(f"ps{i}", [P, 2, 512], F32)) for i in range(4)]
        m.x1_dram = nc.dram_tensor("x1_dram", (rows, D), F32, kind="Internal").ap()
        m.acc_dram = [nc.dram_tensor(f"acc_dram{j}", (rows, D), F32, kind="Internal").ap() for j in range(NACC)]
        m.shift_dram = [nc.dram_tensor(f"shift_dram{j}", (T, T + 1), F32, kind="Internal").ap() for j in range(4)]
        m.stack_dram = [nc.dram_tensor(f"stack_dram{j}", (16 * 48, T), mybir.dt.bfloat16, kind="Internal").ap()
                        for j in range(3)]
        make_constants(m)
        m.token = m.sb("token", [P, 48], U32)
        m.share = m.sb("share", [P, 48])

        x1 = m.sb("x1", [P, NTT, D])
        zeros = m.sb("zeros", [P, D])
        z = m.memset(m.pool, zeros[:, :], 0.0)
        l_zero = m.lane("l_zero")

        def zero_accumulator(j):
            for q in range(NTT // 4):
                m.zeroed = m.sp.dma(l_zero, m.acc_dram[j][q * 4 * P:(q + 1) * 4 * P, :]
                                    .rearrange("(p n) d -> p n d", p=P),
                                    zeros[:, :].unsqueeze(1).broadcast_to([P, 4, D]), z)

        m.zero_accumulator = zero_accumulator
        with ExitStack() as m.stage_ctx:
            m.stage("dist")
            distance_attention(m, part("L0_attn_"), x1)
            m.close_stage()
        with ExitStack() as m.stage_ctx:
            m.stage("route")
            relative = relative_attention(m, dict(part("L1_attn_"), peT=ins["peT"]), part("L1_ffn_"), out, x1)
            next(relative)
            layer_ctx = m.stage_ctx
            with ExitStack() as m.stage_ctx:
                experts_run = experts(m, part("L0_ffn_"), lambda: next(relative))
                route(m, part("L0_ffn_"), x1, lambda: next(experts_run))
                m.stage("experts")
                next(experts_run)
                m.close_stage()
            m.stage_ctx = layer_ctx
            m.stage("rel")
            next(relative, None)
            m.sp.wait(m.final)

        with nc.Block() as block:
            block.sync(lambda e: m.sp.play(e))
            block.gpsimd(lambda e: m.pool.play(e))
            block.scalar(lambda e: m.act.play(e))
            block.vector(lambda e: m.dve.play(e))
            block.tensor(lambda e: m.pe.play(e))


_INS = ["L0_attn_X", "L0_attn_W_in", "L0_attn_b_in", "L0_attn_W_out", "L0_attn_b_out", "L0_ffn_Wr", "L0_ffn_W1",
        "L0_ffn_b1", "L0_ffn_W2", "L0_ffn_b2", "L1_attn_ln_g", "L1_attn_ln_b", "L1_attn_Wq", "L1_attn_bq",
        "L1_attn_Wk", "L1_attn_bk", "L1_attn_Wv", "L1_attn_bv", "L1_attn_Wp", "L1_attn_Wo", "L1_attn_bo",
        "L1_attn_u_bias", "L1_attn_v_bias", "L1_ffn_gate_w", "L1_ffn_w0", "L1_ffn_b0", "L1_ffn_w1", "L1_ffn_b1"]


def position_table(length, width):
    pos = np.arange(length, dtype=np.float32)[:, None]
    div = np.exp(np.arange(0, width, 2, dtype=np.float32) * np.float32(-np.log(10000.0) / width)).astype(np.float32)
    ang = (pos * div).astype(np.float32)
    pe = np.stack([np.sin(ang), np.cos(ang)], axis=-1).reshape(length, width).astype(np.float32)
    return np.ascontiguousarray(pe.T)


def kernel(**inputs):
    import concourse.bacc as _bacc
    from concourse.bass_utils import run_bass_kernel_spmd as _run

    nc = _bacc.Bacc("TRN2", target_bir_lowering=False, num_devices=1)
    arrays, args = {}, {}
    for name in _INS:
        a = np.ascontiguousarray(inputs[name])
        arrays[f"in_{name}"] = a
        args[name] = nc.dram_tensor(f"in_{name}", a.shape, mybir.dt.from_np(a.dtype), kind="ExternalInput").ap()
    shape = tuple(inputs["L0_attn_X"].shape)
    peT = position_table(shape[1], shape[2])
    arrays["in_peT"] = peT
    args["peT"] = nc.dram_tensor("in_peT", peT.shape, F32, kind="ExternalInput").ap()
    out = nc.dram_tensor("out", shape, F32, kind="ExternalOutput").ap()
    two_layers_kernel(nc, args, out)
    r = _run(nc, [arrays], core_ids=[0])
    return r.results[0]["out"]
```
